# Optimizing a Trainium2 kernel written in Bass

```python
import numpy as np
import jax
import jax.numpy as jnp

def _softmax(x, axis=-1):
    return jax.nn.softmax(x, axis=axis)

def _gelu(x):
    return jax.nn.gelu(x, approximate=True)

def _silu(x):
    return jax.nn.silu(x)

def _sigmoid(x):
    return jax.nn.sigmoid(x)

def _layernorm(x, axis=-1, eps=1e-05):
    m = jnp.mean(x, axis=axis, keepdims=True)
    v = jnp.var(x, axis=axis, keepdims=True)
    return (x - m) / jnp.sqrt(v + eps)

def _scatter_add(tgt, idx, src, axis=0):
    return tgt.at[idx].add(src)

def _segment_sum(src, seg, n):
    return jax.ops.segment_sum(src, seg, n)
kernel_name = 'mk_cond_seq_d2_seqx_r2_87fb6e'

def setup_inputs(seed: int=0):
    np.random.seed(seed)
    _w = jnp.asarray

    def _rec_inputs():
        import jax
        import jax.numpy as jnp
        _rk = jax.random.key(seed)
        x = 7.22e-05 + 1 * jax.random.normal(jax.random.fold_in(_rk, 1), (8, 512, 512), jnp.float32)
        _lenS = 512 - jax.random.randint(jax.random.fold_in(_rk, 7), (8,), 0, max(1, 512 // 4) + 1, jnp.int32)
        _lenS2 = 512 - jax.random.randint(jax.random.fold_in(_rk, 8), (8,), 0, max(1, 512 // 4) + 1, jnp.int32)
        cond_2048 = 0.00782532 + 1.00527 * jax.random.normal(jax.random.fold_in(_rk, 11), (8, 1024), jnp.float32)
        _validS = jnp.arange(512)[None, :] < _lenS[:, None]
        _validS2 = jnp.arange(512)[None, :] < _lenS2[:, None]
        _causal = jnp.tril(jnp.ones((512, 512), dtype=bool))
        mask_BxSx1_fk1 = jnp.where(jnp.ones((8, 512, 1), dtype=bool), 1.0, 0.0).astype(jnp.float32)
        mask_BxS_ik0 = jnp.where(jnp.broadcast_to(_validS[:, :], (8, 512)), 0, 1).astype(jnp.int32)
        return (x, cond_2048, mask_BxSx1_fk1, mask_BxS_ik0)
    x, cond_2048, mask_BxSx1_fk1, mask_BxS_ik0 = _rec_inputs()

    def _L0_cond_setup():
        import jax, jax.numpy as jnp
        import numpy as np
        B, T, D, H, TE = (4, 1024, 512, 8, 1024)
        EPS = 1e-05

        def _ln(x, w, b):
            m = jnp.mean(x, axis=-1, keepdims=True)
            v = jnp.mean((x - m) ** 2, axis=-1, keepdims=True)
            return (x - m) * jax.lax.rsqrt(v + EPS) * w + b
        key = jax.random.key(seed)
        ks = jax.random.split(key, 16)
        s = 0.02
        inp = {'x': jax.random.normal(ks[0], (B, T, D), jnp.float32), 'emb': jax.random.normal(ks[1], (B, TE), jnp.float32), 'src_mask': (jax.random.uniform(ks[2], (B, T, 1)) > 0.2).astype(jnp.float32), 'num_head': H, 'ln_w': jnp.ones((D,), jnp.float32), 'ln_b': jnp.zeros((D,), jnp.float32), 'Wq': jax.random.normal(ks[3], (D, D), jnp.float32) * s, 'bq': jnp.zeros((D,), jnp.float32), 'Wk': jax.random.normal(ks[4], (D, D), jnp.float32) * s, 'bk': jnp.zeros((D,), jnp.float32), 'Wv': jax.random.normal(ks[5], (D, D), jnp.float32) * s, 'bv': jnp.zeros((D,), jnp.float32), 'W_emb': jax.random.normal(ks[6], (TE, 2 * D), jnp.float32) * s, 'b_emb': jnp.zeros((2 * D,), jnp.float32), 'ln2_w': jnp.ones((D,), jnp.float32), 'ln2_b': jnp.zeros((D,), jnp.float32), 'W_out': jax.random.normal(ks[7], (D, D), jnp.float32) * s, 'b_out': jnp.zeros((D,), jnp.float32)}
        return inp
    _L0_cond_all = _L0_cond_setup()
    _L0_cond_in = {k: v for k, v in _L0_cond_all.items() if k in ('ln_w', 'ln_b', 'Wq', 'bq', 'Wk', 'bk', 'Wv', 'bv', 'W_emb', 'b_emb', 'ln2_w', 'ln2_b', 'W_out', 'b_out')}
    del _L0_cond_all

    def _L1_cond_setup():
        import jax, jax.numpy as jnp
        import numpy as np
        H = 16
        LN_EPS = 1e-05

        def _layernorm(x, scale, bias):
            mu = jnp.mean(x, axis=-1, keepdims=True)
            var = jnp.var(x, axis=-1, keepdims=True)
            return (x - mu) * jax.lax.rsqrt(var + LN_EPS) * scale + bias
        key = jax.random.key(seed)
        ks = jax.random.split(key, 8)
        B, T, D, E = (4, 2048, 512, 1024)
        s = 0.02
        return {'x': jax.random.normal(ks[0], (B, T, D), jnp.float32), 'emb': jax.random.normal(ks[1], (B, E), jnp.float32), 'src_mask': jax.random.randint(ks[2], (B, T), 0, 2).astype(jnp.int32), 'norm_scale': jnp.ones((D,), jnp.float32), 'norm_bias': jnp.zeros((D,), jnp.float32), 'Wq': jax.random.normal(ks[3], (D, D), jnp.float32) * s, 'bq': jnp.zeros((D,), jnp.float32), 'Wk': jax.random.normal(ks[4], (D, D), jnp.float32) * s, 'bk': jnp.zeros((D,), jnp.float32), 'Wv': jax.random.normal(ks[5], (D, D), jnp.float32) * s, 'bv': jnp.zeros((D,), jnp.float32), 'film_emb_W': jax.random.normal(ks[6], (E, 2 * D), jnp.float32) * s, 'film_emb_b': jnp.zeros((2 * D,), jnp.float32), 'film_norm_scale': jnp.ones((D,), jnp.float32), 'film_norm_bias': jnp.zeros((D,), jnp.float32), 'film_out_W': jax.random.normal(ks[7], (D, D), jnp.float32) * s, 'film_out_b': jnp.zeros((D,), jnp.float32)}
    _L1_cond_all = _L1_cond_setup()
    _L1_cond_in = {k: v for k, v in _L1_cond_all.items() if k in ('norm_scale', 'norm_bias', 'Wq', 'bq', 'Wk', 'bk', 'Wv', 'bv', 'film_emb_W', 'film_emb_b', 'film_norm_scale', 'film_norm_bias', 'film_out_W', 'film_out_b')}
    del _L1_cond_all
    return {'x': x, 'cond_2048': cond_2048, 'mask_BxSx1_fk1': mask_BxSx1_fk1, 'mask_BxS_ik0': mask_BxS_ik0, 'L0_cond_ln_w': _L0_cond_in['ln_w'], 'L0_cond_ln_b': _L0_cond_in['ln_b'], 'L0_cond_Wq': _L0_cond_in['Wq'], 'L0_cond_bq': _L0_cond_in['bq'], 'L0_cond_Wk': _L0_cond_in['Wk'], 'L0_cond_bk': _L0_cond_in['bk'], 'L0_cond_Wv': _L0_cond_in['Wv'], 'L0_cond_bv': _L0_cond_in['bv'], 'L0_cond_W_emb': _L0_cond_in['W_emb'], 'L0_cond_b_emb': _L0_cond_in['b_emb'], 'L0_cond_ln2_w': _L0_cond_in['ln2_w'], 'L0_cond_ln2_b': _L0_cond_in['ln2_b'], 'L0_cond_W_out': _L0_cond_in['W_out'], 'L0_cond_b_out': _L0_cond_in['b_out'], 'L1_cond_norm_scale': _L1_cond_in['norm_scale'], 'L1_cond_norm_bias': _L1_cond_in['norm_bias'], 'L1_cond_Wq': _L1_cond_in['Wq'], 'L1_cond_bq': _L1_cond_in['bq'], 'L1_cond_Wk': _L1_cond_in['Wk'], 'L1_cond_bk': _L1_cond_in['bk'], 'L1_cond_Wv': _L1_cond_in['Wv'], 'L1_cond_bv': _L1_cond_in['bv'], 'L1_cond_film_emb_W': _L1_cond_in['film_emb_W'], 'L1_cond_film_emb_b': _L1_cond_in['film_emb_b'], 'L1_cond_film_norm_scale': _L1_cond_in['film_norm_scale'], 'L1_cond_film_norm_bias': _L1_cond_in['film_norm_bias'], 'L1_cond_film_out_W': _L1_cond_in['film_out_W'], 'L1_cond_film_out_b': _L1_cond_in['film_out_b']}

def reference(x, cond_2048, mask_BxSx1_fk1, mask_BxS_ik0, L0_cond_ln_w, L0_cond_ln_b, L0_cond_Wq, L0_cond_bq, L0_cond_Wk, L0_cond_bk, L0_cond_Wv, L0_cond_bv, L0_cond_W_emb, L0_cond_b_emb, L0_cond_ln2_w, L0_cond_ln2_b, L0_cond_W_out, L0_cond_b_out, L1_cond_norm_scale, L1_cond_norm_bias, L1_cond_Wq, L1_cond_bq, L1_cond_Wk, L1_cond_bk, L1_cond_Wv, L1_cond_bv, L1_cond_film_emb_W, L1_cond_film_emb_b, L1_cond_film_norm_scale, L1_cond_film_norm_bias, L1_cond_film_out_W, L1_cond_film_out_b):
    import jax
    import jax.numpy as jnp

    def _L0_cond_ref(x, emb, src_mask, num_head, ln_w, ln_b, Wq, bq, Wk, bk, Wv, bv, W_emb, b_emb, ln2_w, ln2_b, W_out, b_out):
        import jax, jax.numpy as jnp
        import numpy as np
        B, T, D, H, TE = (4, 1024, 512, 8, 1024)
        EPS = 1e-05

        def _ln(x, w, b):
            m = jnp.mean(x, axis=-1, keepdims=True)
            v = jnp.mean((x - m) ** 2, axis=-1, keepdims=True)
            return (x - m) * jax.lax.rsqrt(v + EPS) * w + b
        b, t, d = x.shape
        h = num_head
        dh = d // h
        xn = _ln(x, ln_w, ln_b)
        q = xn @ Wq + bq
        k = xn @ Wk + bk + (1.0 - src_mask) * -1000000.0
        q = jax.nn.softmax(q.reshape(b, t, h, dh), axis=-1)
        k = jax.nn.softmax(k.reshape(b, t, h, dh), axis=1)
        v = ((xn @ Wv + bv) * src_mask).reshape(b, t, h, dh)
        att = jnp.einsum('bnhd,bnhl->bhdl', k, v)
        y = jnp.einsum('bnhd,bhdl->bnhl', q, att).reshape(b, t, d)
        emb_out = (jax.nn.silu(emb) @ W_emb + b_emb)[:, None, :]
        scale, shift = jnp.split(emb_out, 2, axis=2)
        hh = _ln(y, ln2_w, ln2_b) * (1.0 + scale) + shift
        hh = jax.nn.silu(hh) @ W_out + b_out
        return x + hh

    def _L1_cond_ref(x, emb, src_mask, norm_scale, norm_bias, Wq, bq, Wk, bk, Wv, bv, film_emb_W, film_emb_b, film_norm_scale, film_norm_bias, film_out_W, film_out_b):
        import jax, jax.numpy as jnp
        import numpy as np
        H = 16
        LN_EPS = 1e-05

        def _layernorm(x, scale, bias):
            mu = jnp.mean(x, axis=-1, keepdims=True)
            var = jnp.var(x, axis=-1, keepdims=True)
            return (x - mu) * jax.lax.rsqrt(var + LN_EPS) * scale + bias
        B, T, D = x.shape
        dh = D // H
        xn = _layernorm(x, norm_scale, norm_bias)
        q = xn @ Wq + bq
        k = xn @ Wk + bk
        v = xn @ Wv + bv
        mask = (src_mask == 1)[:, :, None]
        k = jnp.where(mask, -jnp.inf, k)
        v = jnp.where(mask, 0.0, v)
        q = q.reshape(B, T, H, dh).transpose(0, 2, 1, 3)
        k = k.reshape(B, T, H, dh).transpose(0, 2, 1, 3)
        v = v.reshape(B, T, H, dh).transpose(0, 2, 1, 3)
        q = jax.nn.softmax(q, axis=-1)
        k = jax.nn.softmax(k, axis=2)
        attn = jnp.einsum('bhse,bhsd->bhed', k, v)
        y = jnp.einsum('bhtd,bhed->bhte', q, attn)
        y = y.transpose(0, 2, 1, 3).reshape(B, T, D)
        emb_out = jax.nn.silu(emb) @ film_emb_W + film_emb_b
        scale, shift = jnp.split(emb_out, 2, axis=-1)
        h = _layernorm(y, film_norm_scale, film_norm_bias) * (1.0 + scale[:, None, :]) + shift[:, None, :]
        h = jax.nn.silu(h) @ film_out_W + film_out_b
        return x + h
    x = _L0_cond_ref(x, cond_2048, mask_BxSx1_fk1, 8, L0_cond_ln_w, L0_cond_ln_b, L0_cond_Wq, L0_cond_bq, L0_cond_Wk, L0_cond_bk, L0_cond_Wv, L0_cond_bv, L0_cond_W_emb, L0_cond_b_emb, L0_cond_ln2_w, L0_cond_ln2_b, L0_cond_W_out, L0_cond_b_out)
    x = _L1_cond_ref(x, cond_2048, mask_BxS_ik0, L1_cond_norm_scale, L1_cond_norm_bias, L1_cond_Wq, L1_cond_bq, L1_cond_Wk, L1_cond_bk, L1_cond_Wv, L1_cond_bv, L1_cond_film_emb_W, L1_cond_film_emb_b, L1_cond_film_norm_scale, L1_cond_film_norm_bias, L1_cond_film_out_W, L1_cond_film_out_b)
    return x

_drawn_inputs = setup_inputs


def setup_inputs(seed=0):
    import zlib

    import numpy as np

    out = dict(_drawn_inputs(seed))
    spreads = {'L0_cond_ln_w': (1.0, 0.6),
     'L0_cond_ln_b': (0.0, 0.1),
     'L0_cond_bq': (0.0, 0.8),
     'L0_cond_bk': (0.0, 2.0),
     'L0_cond_bv': (0.0, 0.1),
     'L0_cond_b_emb': (0.0, 0.1),
     'L0_cond_ln2_w': (1.0, 0.2),
     'L0_cond_ln2_b': (0.0, 0.1),
     'L0_cond_b_out': (0.0, 0.1),
     'L1_cond_norm_scale': (1.0, 0.2),
     'L1_cond_norm_bias': (0.0, 0.1),
     'L1_cond_bq': (0.0, 0.296),
     'L1_cond_bk': (0.0, 2.0),
     'L1_cond_bv': (0.0, 0.1),
     'L1_cond_film_emb_b': (0.0, 0.1),
     'L1_cond_film_norm_scale': (1.0, 0.2),
     'L1_cond_film_norm_bias': (0.0, 0.305),
     'L1_cond_film_out_b': (0.0, 0.1)}
    factors = {'L0_cond_Wq': 8.0, 'L0_cond_Wk': 8.0}
    for name, (base, spread) in spreads.items():
        noise = np.random.default_rng([zlib.crc32(name.encode()), seed]).standard_normal(out[name].shape)
        drawn = base * np.exp(spread * noise) if base else spread * noise
        out[name] = jnp.asarray(drawn.astype(out[name].dtype))
    for name, factor in factors.items():
        out[name] = (out[name] * factor).astype(out[name].dtype)
    return out
```

```python
from contextlib import ExitStack

import concourse.bass as bass
from concourse import mybir

P = 128
LAYERS = 2
B, S, D, E = 8, 512, 512, 1024
T = S // P
C = D // P
KE = E // P
UNITS = LAYERS * B
HEADS = (8, 16)
EPS = 1e-5
RING = 6
X_SCALE = 2.0**11
NORM_MAX = float(D) ** 0.5 * 1.001
MASK_ADD = 1e6
MASKED_OUT = -3e38
EXP_BITS = 0x7F800000
TINY = 2.0**-60

F32 = mybir.dt.float32
F16 = mybir.dt.float16
I32 = mybir.dt.int32
ALU = mybir.AluOpType
ACT = mybir.ActivationFunctionType
AX_X = mybir.AxisListType.X
RMAX = bass.bass_isa.ReduceOp.max

LN_W, LN_B, B_K, LN2_W, LN2_B, B_EMB = 0, 4, 8, 12, 16, 20
COLS = 28

STAGES = [("K", 0), ("YT", -1), ("V", 0), ("KT", 0), ("Q", 0), ("XT", 1), ("O", -1), ("QT", 0), ("Y", 0)]
OFFSET = dict(STAGES)
SLOTS = [(name, i) for name, _ in STAGES for i in range(4)]
assert len(SLOTS) % RING == 0


def exists(name, u):
    if not isinstance(u, int):
        return True
    return 0 <= u + OFFSET[name] < UNITS


def previous_user(name, i, u):
    j = SLOTS.index((name, i))
    while True:
        j -= RING
        if j < 0:
            j, u = j + len(SLOTS), u - 1
            if isinstance(u, int) and u < -1:
                return None
        before, n = SLOTS[j]
        if exists(before, u):
            return before, n, u + OFFSET[before]


def build(nc, x_d, emb_d, mask0_d, mask1_d, maskcol0_d, maskcol1_d, w_d, bias_d, wemb_d, cols_d, ident_d, blocks_d, out_d):
    with ExitStack() as ctx:
        def sb(name, shape, dt):
            return ctx.enter_context(nc.sbuf_tensor("sb_" + name, shape, dt))

        def sem(name):
            return ctx.enter_context(nc.semaphore(name))

        x = sb("x", [P, B * T, D], F32)
        w_hi = [sb(f"w_hi{i}", [P, C, D], F16) for i in range(5)]
        w_lo = [sb(f"w_lo{i}", [P, C, D], F16) for i in range(5)]
        w_stage = sb("w_stage", [P, C, D], F32)
        xh_or_h = sb("xh_or_h", [P, T, D], F32)
        k_or_qt = sb("k_or_qt", [P, C, S], F32)
        kt_or_y = sb("kt_or_y", [P, T, D], F32)
        v = sb("v", [P, T, D], F32)
        q = sb("q", [P, T, D], F32)
        xt_hi = sb("xt_hi", [P, C, S], F16)
        xt_lo = sb("xt_lo", [P, C, S], F16)
        ht_hi = sb("ht_hi", [P, C, S], F16)
        ht_lo = sb("ht_lo", [P, C, S], F16)
        att = sb("att", [P, C, P], F32)
        tanh = sb("tanh", [P, 2, S], F32)
        mask_raw = sb("mask_raw", [P, S], F32)
        mask_add = sb("mask_add", [P, S], F32)
        bias_q = [sb(f"bias_q{i}", [P, D], F32) for i in range(LAYERS)]
        bias_v = [sb(f"bias_v{i}", [P, D], F32) for i in range(LAYERS)]
        bias_o = [sb(f"bias_o{i}", [P, D], F32) for i in range(LAYERS)]
        bias_k = sb("bias_k", [P, LAYERS, C], F32)
        wemb = sb("wemb", [P, 2, KE, P], F32)
        cols = sb("cols", [P, LAYERS, COLS], F32)
        lnb_wide = sb("lnb_wide", [P, C, P], F32)
        ident = sb("ident", [P, P], F32)
        blocks = sb("blocks", [P, LAYERS, P], F32)
        film = [sb(f"film{i}", [P, B, 4, C], F32) for i in range(LAYERS)]
        film_now = sb("film_now", [P, 4, C], F32)
        mask_cols = sb("mask_cols", [P, LAYERS, B, T], F32)
        mask_int = sb("mask_int", [P, B, T], I32)
        mask_now = sb("mask_now", [P, T], F32)
        emb = sb("emb", [P, KE, B], F32)
        emb_half = sb("emb_half", [P, KE, B], F32)
        emb_tanh = sb("emb_tanh", [P, KE, B], F32)
        film_f = sb("film_f", [P, 2 * C, B], F32)
        film_g = sb("film_g", [P, C, B], F32)
        film_s = sb("film_s", [P, C, B], F32)
        peak = sb("peak", [P, LAYERS, 8], F32)
        peak_all = sb("peak_all", [P, LAYERS, 8], F32)
        scale_up = sb("scale_up", [P, LAYERS, 8], F32)
        scale_down = sb("scale_down", [P, LAYERS, 8], F32)
        down_o = sb("down_o", [P, LAYERS], F32)
        mask_scale = sb("mask_scale", [P, 1], F32)
        k_max = sb("k_max", [P, C], F32)
        k_top = sb("k_top", [P, C], F32)
        k_shift = sb("k_shift", [P, C], F32)
        k_sum = sb("k_sum", [P, C], F32)
        k_recip = sb("k_recip", [P, C], F32)
        q_max = sb("q_max", [P, T, max(HEADS)], F32)
        q_sum = sb("q_sum", [P, T, max(HEADS)], F32)
        q_recip = sb("q_recip", [P, T, max(HEADS)], F32)
        minus_half = sb("minus_half", [P, T], F32)
        x_stats = sb("x_stats", [P, T, 6], F32)
        x_mean_var = sb("x_mean_var", [P, T, 2], F32)
        x_var = sb("x_var", [P, T], F32)
        x_rstd = sb("x_rstd", [P, T], F32)
        x_mul = sb("x_mul", [P, T], F32)
        x_add = sb("x_add", [P, T], F32)
        y_stats = sb("y_stats", [P, T, 6], F32)
        y_mean_var = sb("y_mean_var", [P, T, 2], F32)
        y_var = sb("y_var", [P, T], F32)
        y_rstd = sb("y_rstd", [P, T], F32)
        y_add = sb("y_add", [P, T], F32)
        spare = sb("spare", [P, 6], F32)
        ring = [ctx.enter_context(nc.psum_tensor(f"ring{i}", [P, 512], F32)) for i in range(RING)]
        att_ps = ctx.enter_context(nc.psum_tensor("att_ps", [P, C, P], F32))
        prep_ps = ctx.enter_context(nc.psum_tensor("prep_ps", [P, 512], F32))

        def bank(name, i):
            return ring[SLOTS.index((name, i)) % RING][:]

        def xu(b):
            return x[:, bass.ds(b * T, T), :] if not isinstance(b, int) else x[:, b * T:b * T + T, :]

        def xt(b, t):
            return x[:, bass.ds(b * T + t, 1), :].squeeze(1) if not isinstance(b, int) else x[:, b * T + t, :]

        def batch(unit, layer):
            return unit - layer * B

        K_, V_, Q_, O_ = range(4)
        HELD = ((0, 1, 2, 3), (4, 0, 1, 2))
        stages = ((w_stage, kt_or_y, v, q), (w_stage,) * 4)

        x0_loaded, x_loaded = sem("x0_loaded"), sem("x_loaded")
        cols_loaded = sem("cols_loaded")
        row_bias_loaded = [sem(f"row_bias_loaded{i}") for i in range(LAYERS)]
        w_loaded = [sem(f"w_loaded{i}") for i in range(4)]
        wemb_loaded = [sem(f"wemb_loaded{i}") for i in range(2)]
        mask_loaded = sem("mask_loaded")
        out_stored = sem("out_stored")
        done = {name: sem("pe_" + name) for name, _ in STAGES}
        att_summed = sem("att_summed")
        bias_summed, film_summed = sem("bias_summed"), sem("film_summed")
        k_masked, film_read, v_ready, kt_ready = sem("k_masked"), sem("film_read"), sem("v_ready"), sem("kt_ready")
        q_biased, xt_lo_ready, x_new, qt_ready = sem("q_biased"), sem("xt_lo_ready"), sem("x_new"), sem("qt_ready")
        y_ready = sem("y_ready")
        FREES = {"K": k_masked, "YT": film_read, "V": v_ready, "KT": kt_ready, "Q": q_biased, "XT": xt_lo_ready,
                 "O": x_new, "QT": qt_ready, "Y": y_ready}
        att_ready, bias_read, film_ps_read = sem("att_ready"), sem("bias_read"), sem("film_ps_read")
        mask_ready, mask_now_ready, film_now_ready = sem("mask_ready"), sem("mask_now_ready"), sem("film_now_ready")
        k_normed = sem("k_normed")
        k_top_ready, k_shift_ready, k_exp, k_recip_ready = sem("k_top_ready"), sem("k_shift_ready"), sem("k_exp"), sem("k_recip_ready")
        q_max_ready, q_centred, q_exp, q_summed, q_recip_ready = (
            sem("q_max_ready"), sem("q_centred"), sem("q_exp"), sem("q_summed"), sem("q_recip_ready"))
        x_stats_ready, x_mv_ready, x_var_ready, x_rstd_ready, x_affine_ready = (
            sem("x_stats_ready"), sem("x_mv_ready"), sem("x_var_ready"), sem("x_rstd_ready"), sem("x_affine_ready"))
        y_stats_ready, y_mv_ready, y_var_ready, y_rstd_ready, y_affine_ready = (
            sem("y_stats_ready"), sem("y_mv_ready"), sem("y_var_ready"), sem("y_rstd_ready"), sem("y_affine_ready"))
        xh_ready, yh_ready, xt_hi_ready = sem("xh_ready"), sem("yh_ready"), sem("xt_hi_ready")
        h_ready, ht_hi_ready, ht_lo_ready, x_biased = sem("h_ready"), sem("ht_hi_ready"), sem("ht_lo_ready"), sem("x_biased")
        w_weighted, w_peak, w_peak_all, w_scale, w_hi_ready, w_ready = (
            sem("w_weighted"), sem("w_peak"), sem("w_peak_all"), sem("w_scale"), sem("w_hi_ready"), sem("w_ready"))
        film_peak, film_peak_all = sem("film_peak"), sem("film_peak_all")
        consts_ready, emb_tanh_ready, emb_ready = sem("consts_ready"), sem("emb_tanh_ready"), sem("emb_ready")
        dve_chain = sem("dve_chain")

        block = ctx.enter_context(nc.Block())

        @block.sync
        def _(sp):
            def load_mask(layer, b):
                src = (mask0_d, mask1_d)[layer]
                row = src[b:b + 1, :] if isinstance(b, int) else src[bass.ds(b, 1), :]
                dst = mask_raw[:] if layer == 0 else mask_raw[:].bitcast(I32)
                sp.dma_start(dst, row.broadcast_to([P, S])).then_inc(mask_loaded, 16)

            def load_w(layer, m):
                if layer and m:
                    sp.wait_ge(w_ready, 4 * layer + m)
                sp.dma_start(stages[layer][m][:], w_d[layer][m].rearrange("(c p) n -> p c n", p=P)).then_inc(w_loaded[m], 16)

            def load_row_biases(layer):
                for dst, src in zip((bias_v, bias_q, bias_o), bias_d[layer]):
                    sp.dma_start(dst[layer][:], src.rearrange("(a d) -> a d", a=1).broadcast_to([P, D])).then_inc(
                        row_bias_loaded[layer], 16)

            def load_wemb(layer):
                for j in range(2 * C):
                    if layer or j >= 2:
                        sp.wait_ge(film_summed, 2 * C * layer + j - 1)
                    sp.dma_start(wemb[:, j % 2], wemb_d[layer].rearrange("(k p) n -> p k n", p=P)[:, :, j * P:j * P + P]
                                 ).then_inc(wemb_loaded[j % 2], 16)

            def step(u, back, following):
                if following is not None:
                    sp.wait_ge(mask_ready, u + 1)
                    load_mask(following, batch(u + 1, following))
                if back == 1:
                    sp.wait_ge(x_new, 4 * u)
                    store(batch(u - 1, 1))

            def store(b):
                dst = out_d[b] if isinstance(b, int) else out_d[bass.ds(b, 1)].squeeze(0)
                sp.dma_start(dst.rearrange("(t p) d -> p t d", p=P), xu(b)).then_inc(out_stored, 16)

            sp.dma_start(xu(0), x_d[0].rearrange("(t p) d -> p t d", p=P)).then_inc(x0_loaded, 16)
            sp.dma_start(ident[:], ident_d).then_inc(cols_loaded, 16)
            sp.dma_start(cols[:], cols_d).then_inc(cols_loaded, 16)
            sp.dma_start(blocks[:], blocks_d).then_inc(cols_loaded, 16)
            sp.dma_start(mask_cols[:, 0], maskcol0_d).then_inc(cols_loaded, 16)
            sp.dma_start(mask_int[:], maskcol1_d).then_inc(cols_loaded, 16)
            sp.dma_start(emb[:], emb_d).then_inc(cols_loaded, 16)
            for m in range(4):
                load_w(0, m)
                if m == 0:
                    load_mask(0, 0)
                if m == 1:
                    load_row_biases(0)
            for b in range(1, B):
                sp.dma_start(xu(b), x_d[b].rearrange("(t p) d -> p t d", p=P)).then_inc(x_loaded, 16)
            load_row_biases(1)
            sp.wait_ge(w_ready, 1)
            load_w(1, K_)
            step(0, None, 0)
            load_wemb(0)
            with sp.Fori(1, B - 1) as u:
                step(u, 0, 0)
            step(B - 1, 0, 1)
            for m in (V_, Q_, O_):
                load_w(1, m)
            step(B, 0, 1)
            load_wemb(1)
            with sp.Fori(B + 1, UNITS - 1) as u:
                step(u, 1, 1)
            step(UNITS - 1, 1, None)
            for t in range(T):
                sp.wait_ge(x_new, 4 * (UNITS - 1) + t + 1)
                sp.dma_start(out_d[B - 1, t * P:t * P + P, :], xt(B - 1, t)).then_inc(out_stored, 16)
            sp.wait_ge(out_stored, 16 * (B - 1 + T))

        @block.tensor
        def _(pe):
            def take_bank(name, i, u):
                before = previous_user(name, i, u)
                if before is not None:
                    stage, n, unit = before
                    pe.wait_ge(FREES[stage], 4 * unit + n + 1)
                return bank(name, i)

            def product(out, pairs):
                for n, (lhs, rhs) in enumerate(pairs):
                    last = nc.tensor.matmul(out, lhs, rhs, start=(n == 0), stop=(n == len(pairs) - 1))
                return last

            def split_pairs(lhs_hi, lhs_lo, rhs_hi, rhs_lo):
                return [p for c in range(C) for p in ((lhs_hi(c), rhs_hi(c)), (lhs_hi(c), rhs_lo(c)), (lhs_lo(c), rhs_hi(c)))]

            def project_features(name, u, m, layer):
                hi, lo = w_hi[HELD[layer][m]], w_lo[HELD[layer][m]]
                for i in range(C):
                    f = slice(i * P, i * P + P)
                    out = take_bank(name, i, u)
                    product(out, split_pairs(lambda c: hi[:, c, f], lambda c: lo[:, c, f],
                                             lambda c: xt_hi[:, c, :], lambda c: xt_lo[:, c, :])).then_inc(done[name], 1)

            def project_tokens(name, u, m, layer, a_hi, a_lo):
                hi, lo = w_hi[HELD[layer][m]], w_lo[HELD[layer][m]]
                for i in range(T):
                    s = slice(i * P, i * P + P)
                    out = take_bank(name, i, u)
                    product(out, split_pairs(lambda c: a_hi[:, c, s], lambda c: a_lo[:, c, s],
                                             lambda c: hi[:, c, :], lambda c: lo[:, c, :])).then_inc(done[name], 1)

            def turn(name, i, u, source):
                out = take_bank(name, i, u)
                for j in range(4):
                    last = nc.tensor.transpose(out[:, j * P:j * P + P], source(i, j), ident[:])
                last.then_inc(done[name], 1)

            def turn_x(u):
                for i in range(C):
                    if i == 0:
                        pe.wait_ge(xh_ready, 4 * (u + 2))
                    turn("XT", i, u, lambda c, t: xh_or_h[:, t, c * P:c * P + P])

            def sum_bias(layer, m):
                pe.wait_ge(w_loaded[m], 16 * (layer + 1))
                n = 3 * layer + m
                if m == K_:
                    pe.wait_ge(consts_ready, 2 + layer)
                if n:
                    pe.wait_ge(bias_read, n)
                if layer and m == K_:
                    pe.wait_ge(film_ps_read, layer)
                w = stages[layer][m]
                if m == K_:
                    for i in range(C):
                        last = product(prep_ps[:, i:i + 1], [
                            (w[:, c, i * P:i * P + P], cols[:, layer, LN_B + c:LN_B + c + 1]) for c in range(C)])
                else:
                    last = product(prep_ps[:], [(lnb_wide[:, c, :], w[:, c, :]) for c in range(C)])
                last.then_inc(bias_summed, 1)

            def sum_film(layer):
                if layer == 0:
                    pe.wait_ge(emb_ready, 1)
                pe.wait_ge(bias_read, 3 * (layer + 1))
                for j in range(2 * C):
                    pe.wait_ge(wemb_loaded[j % 2], 16 * (C * layer + j // 2 + 1))
                    product(prep_ps[:, j * B:j * B + B], [(wemb[:, j % 2, k, :], emb[:, k, :]) for k in range(KE)]
                            ).then_inc(film_summed, 1)

            def step(u, front, back, following, prep=None):
                first = prep == "first" or (isinstance(u, int) and u == 0)
                if front is not None:
                    pe.wait_ge(xt_lo_ready, 4 * (u + 1))
                    if first:
                        pe.wait_ge(w_ready, 4 * front + K_ + 1)
                    project_features("K", u, K_, front)
                if prep == 1:
                    sum_bias(1, K_)
                if back is not None:
                    pe.wait_ge(yh_ready, 4 * u)
                    for i in range(C):
                        turn("YT", i, u, lambda c, t: kt_or_y[:, t, c * P:c * P + P])
                if front is not None:
                    if first:
                        pe.wait_ge(w_ready, 4 * front + V_ + 1)
                    project_tokens("V", u, V_, front, xt_hi, xt_lo)
                    if front == 0:
                        pe.wait_ge(k_exp, 4 * (u + 1))
                    else:
                        pe.wait_ge(k_normed, 4 * (batch(u, 1) + 1))
                    for i in range(T):
                        turn("KT", i, u, lambda t, c: k_or_qt[:, c, t * P:t * P + P])
                    if prep == 1:
                        sum_bias(1, V_)
                    if first:
                        pe.wait_ge(w_ready, 4 * front + Q_ + 1)
                    project_tokens("Q", u, Q_, front, xt_hi, xt_lo)
                    pe.wait_ge(kt_ready, 4 * (u + 1))
                    pe.wait_ge(v_ready, 4 * (u + 1))
                    if not isinstance(u, int) or u:
                        pe.wait_ge(att_ready, u)
                    for c in range(C):
                        f = slice(c * P, c * P + P)
                        left, right = (kt_or_y, v) if front == 0 else (v, kt_or_y)
                        last = product(att_ps[:, c, :], [(left[:, t, f], right[:, t, f]) for t in range(T)])
                    last.then_inc(att_summed, 1)
                if following is not None:
                    turn_x(u)
                if prep == 1:
                    sum_bias(1, Q_)
                if back is not None:
                    pe.wait_ge(ht_lo_ready, 4 * u)
                    project_tokens("O", u, O_, back, ht_hi, ht_lo)
                if front is not None:
                    for i in range(T):
                        pe.wait_ge(q_exp, 4 * u + i + 1)
                        turn("QT", i, u, lambda t, c: q[:, t, c * P:c * P + P])
                    pe.wait_ge(att_ready, u + 1)
                    for t in range(T):
                        pe.wait_ge(qt_ready, 4 * u + t + 1)
                        out = take_bank("Y", t, u)
                        for c in range(C):
                            last = nc.tensor.matmul(out[:, c * P:c * P + P], k_or_qt[:, t, c * P:c * P + P], att[:, c, :],
                                                    start=True, stop=True)
                        last.then_inc(done["Y"], 1)

            pe.wait_ge(cols_loaded, 96)
            turn_x(-1)
            for m in (K_, V_, Q_):
                sum_bias(0, m)
            step(0, 0, None, 0)
            sum_film(0)
            pe.wait_ge(w_ready, O_ + 1)
            with pe.Fori(1, B - 1) as u:
                step(u, 0, 0, 0)
            step(B - 1, 0, 0, 1, prep=1)
            step(B, 1, 0, 1, prep="first")
            sum_film(1)
            pe.wait_ge(w_ready, 4 + O_ + 1)
            with pe.Fori(B + 1, UNITS - 1) as u:
                step(u, 1, 1, 1)
            step(UNITS - 1, 1, 1, None)
            step(UNITS, None, 1, None)

        @block.vector
        def _(dve):
            links = [0]

            def link(ins):
                links[0] += 1
                ins.then_inc(dve_chain, 1)
                dve.wait_ge(dve_chain, links[0])

            def powers(layer, n, up, down):
                at = (slice(None), layer, slice(n, n + 1))
                link(nc.vector.tensor_scalar(peak_all[at], peak_all[at], TINY, None, ALU.max))
                link(nc.vector.tensor_scalar(scale_down[at].bitcast(I32), peak_all[at].bitcast(I32), EXP_BITS, None, ALU.bitwise_and))
                link(nc.vector.tensor_scalar(scale_up[at].bitcast(I32), scale_down[at].bitcast(I32), EXP_BITS, None, ALU.bitwise_xor))
                link(nc.vector.tensor_scalar(scale_up[at], scale_up[at], up, None, ALU.mult))
                link(nc.vector.tensor_scalar(scale_down[at], scale_down[at], down, None, ALU.mult))

            def wait_here(semaphore, value, word):
                dve.wait_ge(semaphore, value)
                nc.vector.memset(spare[:, word:word + 1], 0.0)

            def prepare_w(layer, m):
                n = 4 * layer + m
                w = stages[layer][m]
                hi, lo = w_hi[HELD[layer][m]], w_lo[HELD[layer][m]]
                if m != O_:
                    dve.wait_ge(bias_summed, 3 * layer + m + 1)
                    dve.wait_ge(row_bias_loaded[layer], 48)
                    if m == K_:
                        ins = nc.vector.tensor_tensor(bias_k[:, layer, :], prep_ps[:, 0:C], cols[:, layer, B_K:B_K + C], ALU.add)
                    else:
                        row = (None, bias_v, bias_q)[m][layer]
                        ins = nc.vector.tensor_tensor(row[:], prep_ps[:], row[:], ALU.add)
                    ins.then_inc(bias_read, 1)
                dve.wait_ge(w_weighted, n + 1)
                nc.vector.tensor_reduce(peak[:, layer, m:m + 1], w[:].rearrange("p c n -> p (c n)"), AX_X, ALU.max,
                                        apply_absolute_value=True).then_inc(w_peak, 1)
                dve.wait_ge(w_peak_all, n + 1)
                powers(layer, m, 2.0**13, 2.0**-14 if m == O_ else 2.0**-14 / X_SCALE)
                if layer == 0 and m == K_:
                    link(nc.vector.tensor_scalar(mask_scale[:], scale_up[:, 0, K_:K_ + 1], X_SCALE, MASK_ADD, ALU.mult, ALU.mult))
                nc.vector.tensor_copy(peak[:, layer, 7:8], scale_up[:, layer, m:m + 1]).then_inc(w_scale, 1)
                dve.wait_ge(w_hi_ready, n + 1)
                nc.vector.scalar_tensor_tensor(out=lo[:], in0=w[:], scalar=scale_up[:, layer, m:m + 1], in1=hi[:],
                                               op0=ALU.mult, op1=ALU.subtract).then_inc(w_ready, 1)

            def prepare_film(layer):
                wide = lambda at: cols[:, layer, at:at + C].unsqueeze(2).broadcast_to([P, C, B])
                dve.wait_ge(film_summed, 2 * C * (layer + 1))
                ins = nc.vector.tensor_tensor(film_f[:], prep_ps[:, 0:2 * C * B].rearrange("p (j b) -> p j b", b=B),
                                              cols[:, layer, B_EMB:B_EMB + 2 * C].unsqueeze(2).broadcast_to([P, 2 * C, B]), ALU.add)
                ins.then_inc(film_ps_read, 1)
                dve.wait_ge(film_ps_read, layer + 1)
                link(nc.vector.tensor_scalar(film_f[:, 0:C, :], film_f[:, 0:C, :], 1.0, None, ALU.add))
                link(nc.vector.tensor_tensor(film_g[:], film_f[:, 0:C, :], wide(LN2_W), ALU.mult))
                link(nc.vector.tensor_tensor(film_s[:], film_f[:, 0:C, :], wide(LN2_B), ALU.mult))
                link(nc.vector.tensor_tensor(film_s[:], film_s[:], film_f[:, C:2 * C, :], ALU.add))
                link(nc.vector.tensor_reduce(peak[:, layer, 4:5], film_g[:].rearrange("p c b -> p (c b)"), AX_X, ALU.max,
                                             apply_absolute_value=True))
                link(nc.vector.tensor_reduce(peak[:, layer, 5:6], film_s[:].rearrange("p c b -> p (c b)"), AX_X, ALU.max,
                                             apply_absolute_value=True))
                nc.vector.scalar_tensor_tensor(out=peak[:, layer, 6:7], in0=peak[:, layer, 4:5], scalar=NORM_MAX,
                                               in1=peak[:, layer, 5:6], op0=ALU.mult, op1=ALU.add).then_inc(film_peak, 1)
                dve.wait_ge(film_peak_all, layer + 1)
                powers(layer, 6, 2.0**13, 2.0**-14)
                table = lambda kind: film[layer][:, :, kind, :].rearrange("p b c -> p c b")
                up = scale_up[:, layer, 6:7]
                link(nc.vector.tensor_scalar(table(0), film_g[:], 0.5, None, ALU.mult))
                link(nc.vector.tensor_scalar(table(1), film_s[:], 0.5, None, ALU.mult))
                link(nc.vector.tensor_scalar(table(2), film_g[:], 0.5, up, ALU.mult, ALU.mult))
                link(nc.vector.tensor_scalar(table(3), film_s[:], 0.5, up, ALU.mult, ALU.mult))
                link(nc.vector.tensor_tensor(down_o[:, layer:layer + 1], scale_down[:, layer, O_:O_ + 1],
                                             scale_down[:, layer, 6:7], ALU.mult))

            def x_statistics(unit, layer):
                b = batch(unit, layer)
                if layer == 1:
                    dve.wait_ge(x_new, 4 * (b + 1))
                for t in range(T):
                    nc.vector.bn_stats(x_stats[:, t, :], xt(b, t)).then_inc(x_stats_ready, 1)
                wait_here(x_stats_ready, 4 * (unit + 1), 4)
                for t in range(T):
                    nc.vector.bn_aggr(x_mean_var[:, t, :], x_stats[:, t, :]).then_inc(x_mv_ready, 1)
                dve.wait_ge(x_mv_ready, 4 * (unit + 1))
                nc.vector.tensor_scalar(x_var[:], x_mean_var[:, :, 1], EPS, None, ALU.add).then_inc(x_var_ready, 1)

            def x_affine(unit):
                dve.wait_ge(x_rstd_ready, unit + 1)
                nc.vector.tensor_scalar(x_mul[:], x_rstd[:], X_SCALE, None, ALU.mult).then_inc(x_affine_ready, 1)
                nc.vector.scalar_tensor_tensor(out=x_add[:], in0=x_mean_var[:, :, 0], scalar=-X_SCALE, in1=x_rstd[:],
                                               op0=ALU.mult, op1=ALU.mult).then_inc(x_affine_ready, 1)

            def x_low_part(unit):
                for c in range(C):
                    dve.wait_ge(xt_hi_ready, 4 * unit + c + 1)
                    nc.vector.tensor_tensor(xt_lo[:, c, :], bank("XT", c), xt_hi[:, c, :], ALU.subtract).then_inc(xt_lo_ready, 1)

            def step(u, front, back, following, prep=None):
                if back is not None:
                    dve.wait_ge(y_rstd_ready, u)
                    nc.vector.scalar_tensor_tensor(out=y_add[:], in0=y_mean_var[:, :, 0], scalar=-1.0, in1=y_rstd[:],
                                                   op0=ALU.mult, op1=ALU.mult).then_inc(y_affine_ready, 1)
                    b = batch(u - 1, back)
                    src = film[back][:, b] if isinstance(b, int) else film[back][:, bass.ds(b, 1)].squeeze(1)
                    nc.vector.tensor_copy(film_now[:], src).then_inc(film_now_ready, 1)
                if front is not None:
                    heads = HEADS[front]
                    dve.wait_ge(mask_loaded, 16 * (u + 1))
                    if front == 0:
                        nc.vector.tensor_scalar(mask_add[:], mask_raw[:], 1.0, mask_scale[:], ALU.subtract, ALU.mult
                                                ).then_inc(mask_ready, 1)
                    else:
                        nc.vector.tensor_scalar(mask_add[:], mask_raw[:].bitcast(I32), 1.0, MASKED_OUT, ALU.is_equal, ALU.mult
                                                ).then_inc(mask_ready, 1)
                    b = batch(u, front)
                    src = mask_cols[:, front, b] if isinstance(b, int) else mask_cols[:, front, bass.ds(b, 1)].squeeze(1)
                    nc.vector.tensor_copy(mask_now[:], src).then_inc(mask_now_ready, 1)
                    dve.wait_ge(mask_ready, u + 1)
                    for i in range(C):
                        wait_here(done["K"], 4 * u + i + 1, i)
                        nc.vector.tensor_tensor_reduce(k_or_qt[:, i, :], bank("K", i), mask_add[:],
                                                       scale_down[:, front, K_:K_ + 1], -3.4e38, ALU.add, ALU.max,
                                                       k_max[:, i:i + 1]).then_inc(k_masked, 1)
                    dve.wait_ge(k_masked, 4 * (u + 1))
                    nc.vector.tensor_tensor(k_top[:], k_max[:], bias_k[:, front, :], ALU.add).then_inc(k_top_ready, 1)
                    dve.wait_ge(k_top_ready, u + 1)
                    nc.vector.tensor_tensor(k_shift[:], bias_k[:, front, :], k_top[:], ALU.subtract).then_inc(k_shift_ready, 1)
                if prep == 1:
                    prepare_w(1, K_)
                if following is not None:
                    x_statistics(u + 1, following)
                if front is not None:
                    dve.wait_ge(k_exp, 4 * (u + 1))
                    nc.vector.reciprocal(k_recip[:], k_sum[:]).then_inc(k_recip_ready, 1)
                    dve.wait_ge(k_recip_ready, u + 1)
                    if front == 1:
                        for i in range(C):
                            nc.vector.tensor_scalar(k_or_qt[:, i, :], k_or_qt[:, i, :], k_recip[:, i:i + 1], None, ALU.mult
                                                    ).then_inc(k_normed, 1)
                if back is not None:
                    for c in range(C):
                        dve.wait_ge(film_read, 4 * (u - 1) + c + 1)
                        nc.vector.scalar_tensor_tensor(out=xh_or_h[:, c, :], in0=tanh[:, c % 2, :], scalar=1.0,
                                                       in1=xh_or_h[:, c, :], op0=ALU.add, op1=ALU.mult).then_inc(h_ready, 1)
                if front is not None:
                    for t in range(T):
                        dve.wait_ge(done["V"], 4 * u + t + 1)
                        nc.vector.scalar_tensor_tensor(out=v[:, t, :], in0=bank("V", t), scalar=scale_down[:, front, V_:V_ + 1],
                                                       in1=bias_v[front][:], op0=ALU.mult, op1=ALU.add).then_inc(v_ready, 1)
                if prep == 1:
                    prepare_w(1, V_)
                if following is not None:
                    x_affine(u + 1)
                if front is not None:
                    by_head = lambda a: a.rearrange("p (h e) -> p h e", h=heads)
                    wide = lambda a: a.unsqueeze(2).broadcast_to([P, heads, D // heads])
                    for t in range(T):
                        dve.wait_ge(done["Q"], 4 * u + t + 1)
                        nc.vector.scalar_tensor_tensor(out=q[:, t, :], in0=bank("Q", t), scalar=scale_down[:, front, Q_:Q_ + 1],
                                                       in1=bias_q[front][:], op0=ALU.mult, op1=ALU.add).then_inc(q_biased, 1)
                        dve.wait_ge(q_biased, 4 * u + t + 1)
                        nc.vector.tensor_reduce(q_max[:, t, 0:heads], by_head(q[:, t, :]), AX_X, ALU.max).then_inc(q_max_ready, 1)
                        dve.wait_ge(q_max_ready, 4 * u + t + 1)
                        nc.vector.tensor_tensor(by_head(q[:, t, :]), by_head(q[:, t, :]), wide(q_max[:, t, 0:heads]),
                                                ALU.subtract).then_inc(q_centred, 1)
                    dve.wait_ge(att_summed, u + 1)
                    if front == 0:
                        for c in range(C):
                            last = nc.vector.scalar_tensor_tensor(out=att[:, c, :], in0=att_ps[:, c, :],
                                                                  scalar=k_recip[:, c:c + 1], in1=blocks[:, 0, :],
                                                                  op0=ALU.mult, op1=ALU.mult)
                    else:
                        last = nc.vector.tensor_tensor(att[:], att_ps[:], blocks[:, 1:2, :].broadcast_to([P, C, P]), ALU.mult)
                    last.then_inc(att_ready, 1)
                if following is not None:
                    x_low_part(u + 1)
                if prep == 1:
                    prepare_w(1, Q_)
                if front is not None:
                    for t in range(T):
                        dve.wait_ge(q_exp, 4 * u + t + 1)
                        nc.vector.tensor_reduce(q_sum[:, t, 0:heads], by_head(q[:, t, :]), AX_X, ALU.add).then_inc(q_summed, 1)
                    dve.wait_ge(q_summed, 4 * (u + 1))
                    nc.vector.reciprocal(q_recip[:, :, 0:heads], q_sum[:, :, 0:heads]).then_inc(q_recip_ready, 1)
                if back is not None:
                    dve.wait_ge(x_biased, u)
                    b = batch(u - 1, back)
                    for t in range(T):
                        dve.wait_ge(done["O"], 4 * (u - 1) + t + 1)
                        nc.vector.scalar_tensor_tensor(out=xt(b, t), in0=bank("O", t), scalar=down_o[:, back:back + 1],
                                                       in1=xt(b, t), op0=ALU.mult, op1=ALU.add).then_inc(x_new, 1)
                if front is not None:
                    dve.wait_ge(q_recip_ready, u + 1)
                    for t in range(T):
                        dve.wait_ge(done["Y"], 4 * u + t + 1)
                        nc.vector.tensor_tensor(by_head(kt_or_y[:, t, :]), by_head(bank("Y", t)), wide(q_recip[:, t, 0:heads]),
                                                ALU.mult).then_inc(y_ready, 1)
                    for t in range(T):
                        dve.wait_ge(y_ready, 4 * u + t + 1)
                        nc.vector.bn_stats(y_stats[:, t, :], kt_or_y[:, t, :]).then_inc(y_stats_ready, 1)
                    wait_here(y_stats_ready, 4 * (u + 1), 5)
                    for t in range(T):
                        nc.vector.bn_aggr(y_mean_var[:, t, :], y_stats[:, t, :]).then_inc(y_mv_ready, 1)
                    dve.wait_ge(y_mv_ready, 4 * (u + 1))
                    nc.vector.tensor_scalar(y_var[:], y_mean_var[:, :, 1], EPS, None, ALU.add).then_inc(y_var_ready, 1)
                if prep == 1:
                    prepare_w(1, O_)

            def widen_ln_b(layer):
                nc.vector.tensor_copy(lnb_wide[:], cols[:, layer, LN_B:LN_B + C].unsqueeze(2).broadcast_to([P, C, P])
                                      ).then_inc(consts_ready, 1)

            nc.vector.memset(minus_half[:], -0.5).then_inc(consts_ready, 1)
            dve.wait_ge(x0_loaded, 16)
            x_statistics(0, 0)
            dve.wait_ge(cols_loaded, 96)
            widen_ln_b(0)
            x_affine(0)
            link(nc.vector.tensor_scalar(mask_cols[:, 1], mask_int[:], 1.0, None, ALU.not_equal))
            link(nc.vector.tensor_scalar(emb_half[:], emb[:], 0.5, None, ALU.mult))
            x_low_part(0)
            prepare_w(0, K_)
            prepare_w(0, V_)
            prepare_w(0, Q_)
            prepare_w(0, O_)
            dve.wait_ge(emb_tanh_ready, 1)
            nc.vector.scalar_tensor_tensor(out=emb[:], in0=emb_tanh[:], scalar=1.0, in1=emb_half[:], op0=ALU.add, op1=ALU.mult
                                           ).then_inc(emb_ready, 1)
            dve.wait_ge(x_loaded, 16 * (B - 1))
            step(0, 0, None, 0)
            prepare_film(0)
            with dve.Fori(1, B - 1) as u:
                step(u, 0, 0, 0)
            dve.wait_ge(bias_summed, 3)
            widen_ln_b(1)
            step(B - 1, 0, 0, 1, prep=1)
            step(B, 1, 0, 1)
            prepare_film(1)
            with dve.Fori(B + 1, UNITS - 1) as u:
                step(u, 1, 1, 1)
            step(UNITS - 1, 1, 1, None)
            step(UNITS, None, 1, None)

        @block.scalar
        def _(act):
            def prepare_w(layer, m):
                n = 4 * layer + m
                w = stages[layer][m]
                act.wait_ge(w_loaded[m], 16 * (layer + 1))
                if m == O_:
                    act.wait_ge(bias_summed, 3 * (layer + 1))
                    nc.scalar.copy(w[0:1, 0, 0:1], w[0:1, 0, 0:1]).then_inc(w_weighted, 1)
                else:
                    act.wait_ge(bias_summed, 3 * layer + m + 1)
                    for c in range(C):
                        last = nc.scalar.activation(w[:, c, :], w[:, c, :], ACT.Copy,
                                                    scale=cols[:, layer, LN_W + c:LN_W + c + 1])
                    last.then_inc(w_weighted, 1)
                act.wait_ge(w_scale, n + 1)
                if layer == 1 and m != K_:
                    act.wait_ge(done[("K", "V", "Q")[HELD[1][m]]], 4 * B)
                nc.scalar.activation(w_hi[HELD[layer][m]][:], w[:], ACT.Copy, scale=scale_up[:, layer, m:m + 1]).then_inc(w_hi_ready, 1)

            def normalise_x(unit, layer, after_h):
                b = batch(unit, layer)
                act.wait_ge(x_affine_ready, 2 * (unit + 1))
                if after_h is not None:
                    act.wait_ge(ht_lo_ready, 4 * after_h)
                for t in range(T):
                    nc.scalar.activation(xh_or_h[:, t, :], xt(b, t), ACT.Identity, bias=x_add[:, t:t + 1],
                                         scale=x_mul[:, t:t + 1]).then_inc(xh_ready, 1)

            def x_high_part(unit):
                for c in range(C):
                    act.wait_ge(done["XT"], 4 * unit + c + 1)
                    nc.scalar.copy(xt_hi[:, c, :], bank("XT", c)).then_inc(xt_hi_ready, 1)

            def step(u, front, back, following, prep=None):
                if back is not None:
                    act.wait_ge(y_affine_ready, u)
                    for t in range(T):
                        nc.scalar.activation(kt_or_y[:, t, :], kt_or_y[:, t, :], ACT.Identity, bias=y_add[:, t:t + 1],
                                             scale=y_rstd[:, t:t + 1]).then_inc(yh_ready, 1)
                if front is not None:
                    act.wait_ge(k_shift_ready, u + 1)
                    for i in range(C):
                        nc.scalar.activation(k_or_qt[:, i, :], k_or_qt[:, i, :], ACT.Exp, bias=k_shift[:, i:i + 1],
                                             accum_out=k_sum[:, i:i + 1]).then_inc(k_exp, 1)
                if prep == 1:
                    prepare_w(1, K_)
                if back is not None:
                    act.wait_ge(film_now_ready, u)
                    for c in range(C):
                        act.wait_ge(done["YT"], 4 * (u - 1) + c + 1)
                        if c >= 2:
                            act.wait_ge(h_ready, 4 * (u - 1) + c - 1)
                        nc.scalar.activation(tanh[:, c % 2, :], bank("YT", c), ACT.Tanh, bias=film_now[:, 1, c:c + 1],
                                             scale=film_now[:, 0, c:c + 1])
                        nc.scalar.activation(xh_or_h[:, c, :], bank("YT", c), ACT.Identity, bias=film_now[:, 3, c:c + 1],
                                             scale=film_now[:, 2, c:c + 1]).then_inc(film_read, 1)
                    for c in range(C):
                        act.wait_ge(h_ready, 4 * (u - 1) + c + 1)
                        nc.scalar.copy(ht_hi[:, c, :], xh_or_h[:, c, :]).then_inc(ht_hi_ready, 1)
                if front is not None:
                    act.wait_ge(mask_now_ready, u + 1)
                    for t in range(T):
                        act.wait_ge(done["KT"], 4 * u + t + 1)
                        nc.scalar.activation(kt_or_y[:, t, :], bank("KT", t), ACT.Copy, scale=mask_now[:, t:t + 1]
                                             ).then_inc(kt_ready, 1)
                if prep == 1:
                    prepare_w(1, V_)
                if following is not None:
                    normalise_x(u + 1, following, u if back is not None else None)
                if front is not None:
                    for t in range(T):
                        act.wait_ge(q_centred, 4 * u + t + 1)
                        nc.scalar.activation(q[:, t, :], q[:, t, :], ACT.Exp).then_inc(q_exp, 1)
                if following is not None:
                    x_high_part(u + 1)
                if prep == 1:
                    prepare_w(1, Q_)
                if front is not None:
                    for t in range(T):
                        act.wait_ge(done["QT"], 4 * u + t + 1)
                        nc.scalar.copy(k_or_qt[:, t, :], bank("QT", t)).then_inc(qt_ready, 1)
                if prep == 1:
                    prepare_w(1, O_)

            act.wait_ge(x0_loaded, 16)
            act.wait_ge(cols_loaded, 96)
            nc.scalar.activation(emb_tanh[:], emb[:], ACT.Tanh, scale=0.5).then_inc(emb_tanh_ready, 1)
            normalise_x(0, 0, None)
            x_high_part(0)
            for m in range(4):
                prepare_w(0, m)
            step(0, 0, None, 0)
            with act.Fori(1, B - 1) as u:
                step(u, 0, 0, 0)
            step(B - 1, 0, 0, 1, prep=1)
            step(B, 1, 0, 1)
            with act.Fori(B + 1, UNITS - 1) as u:
                step(u, 1, 1, 1)
            step(UNITS - 1, 1, 1, None)
            step(UNITS, None, 1, None)

        @block.gpsimd
        def _(pool):
            def x_power(unit):
                pool.wait_ge(x_var_ready, unit + 1)
                nc.gpsimd.tensor_tensor(x_rstd[:], x_var[:], minus_half[:], ALU.pow).then_inc(x_rstd_ready, 1)

            def add_bias(unit, layer):
                b = batch(unit, layer)
                pool.wait_ge(xh_ready, 4 * (unit + 1))
                nc.gpsimd.tensor_tensor(xu(b), xu(b), bias_o[layer][:].unsqueeze(1).broadcast_to([P, T, D]), ALU.add
                                        ).then_inc(x_biased, 1)

            def prepare_w(layer, m):
                pool.wait_ge(w_peak, 4 * layer + m + 1)
                nc.gpsimd.partition_all_reduce(peak_all[:, layer, m:m + 1], peak[:, layer, m:m + 1], P, RMAX).then_inc(w_peak_all, 1)

            def prepare_film(layer):
                pool.wait_ge(film_peak, layer + 1)
                nc.gpsimd.partition_all_reduce(peak_all[:, layer, 6:7], peak[:, layer, 6:7], P, RMAX).then_inc(film_peak_all, 1)

            def step(u, front, back, following, prep=None):
                if back is not None:
                    pool.wait_ge(y_var_ready, u)
                    nc.gpsimd.tensor_tensor(y_rstd[:], y_var[:], minus_half[:], ALU.pow).then_inc(y_rstd_ready, 1)
                if prep == 1:
                    prepare_w(1, K_)
                if following is not None:
                    x_power(u + 1)
                if back is not None:
                    for c in range(C):
                        pool.wait_ge(ht_hi_ready, 4 * (u - 1) + c + 1)
                        nc.gpsimd.tensor_tensor(ht_lo[:, c, :], xh_or_h[:, c, :], ht_hi[:, c, :], ALU.subtract
                                                ).then_inc(ht_lo_ready, 1)
                if prep == 1:
                    prepare_w(1, V_)
                if following is not None:
                    add_bias(u + 1, following)
                if prep == 1:
                    prepare_w(1, Q_)
                    prepare_w(1, O_)

            pool.wait_ge(consts_ready, 1)
            x_power(0)
            for m in range(4):
                prepare_w(0, m)
            pool.wait_ge(row_bias_loaded[0], 48)
            add_bias(0, 0)
            step(0, 0, None, 0)
            prepare_film(0)
            with pool.Fori(1, B - 1) as u:
                step(u, 0, 0, 0)
            pool.wait_ge(row_bias_loaded[1], 48)
            step(B - 1, 0, 0, 1, prep=1)
            step(B, 1, 0, 1)
            prepare_film(1)
            with pool.Fori(B + 1, UNITS - 1) as u:
                step(u, 1, 1, 1)
            step(UNITS - 1, 1, 1, None)
            step(UNITS, None, 1, None)


_W = (("L0_cond_Wk", "L0_cond_Wv", "L0_cond_Wq", "L0_cond_W_out"),
      ("L1_cond_Wk", "L1_cond_Wv", "L1_cond_Wq", "L1_cond_film_out_W"))
_ROWS = (("L0_cond_bv", "L0_cond_bq", "L0_cond_b_out"),
         ("L1_cond_bv", "L1_cond_bq", "L1_cond_film_out_b"))
_WEMB = ("L0_cond_W_emb", "L1_cond_film_emb_W")
_COLS = (("L0_cond_ln_w", "L0_cond_ln_b", "L0_cond_bk", "L0_cond_ln2_w", "L0_cond_ln2_b", "L0_cond_b_emb"),
         ("L1_cond_norm_scale", "L1_cond_norm_bias", "L1_cond_bk", "L1_cond_film_norm_scale",
          "L1_cond_film_norm_bias", "L1_cond_film_emb_b"))


def kernel(**inputs):
    import numpy as np
    import concourse.bacc as bacc
    from concourse.bass_utils import run_bass_kernel_spmd

    a = {k: np.ascontiguousarray(v) for k, v in inputs.items()}

    def by_partition(rows, n):
        rows = rows.reshape(*rows.shape[:-1], n, P)
        return np.ascontiguousarray(np.moveaxis(rows, -1, 0))

    mask0 = a["mask_BxSx1_fk1"].reshape(B, S)
    mask1 = a["mask_BxS_ik0"].reshape(B, S)
    arrays = {
        "x": a["x"], "mask0": mask0, "mask1": mask1,
        "emb": np.ascontiguousarray(by_partition(a["cond_2048"], KE).transpose(0, 2, 1)),
        "maskcol0": by_partition(mask0, T), "maskcol1": by_partition(mask1, T),
        "cols": np.stack([np.concatenate([by_partition(a[n], a[n].size // P) for n in names], 1) for names in _COLS], 1),
        "ident": np.eye(P, dtype=np.float32),
        "blocks": np.stack([np.kron(np.eye(P * h // D), np.ones((D // h, D // h))) for h in HEADS], 1).astype(np.float32),
    }
    for names in (*_W, *_ROWS, _WEMB):
        for n in names:
            arrays[n] = a[n]
    nc = bacc.Bacc("TRN2", target_bir_lowering=False, num_devices=1)
    arrays = {f"in_{k}": np.ascontiguousarray(v) for k, v in arrays.items()}
    ap = {k[3:]: nc.dram_tensor(k, v.shape, mybir.dt.from_np(v.dtype), kind="ExternalInput").ap() for k, v in arrays.items()}
    out = nc.dram_tensor("out_0", (B, S, D), F32, kind="ExternalOutput").ap()
    build(nc, ap["x"], ap["emb"], ap["mask0"], ap["mask1"], ap["maskcol0"], ap["maskcol1"],
          [[ap[n] for n in names] for names in _W], [[ap[n] for n in names] for names in _ROWS],
          [ap[n] for n in _WEMB], ap["cols"], ap["ident"], ap["blocks"], out)
    r = run_bass_kernel_spmd(nc, [arrays], core_ids=[0])
    return r.results[0]["out_0"]
```

```python
from contextlib import ExitStack

import concourse.bass as bass
from concourse import mybir

P = 128
LAYERS = 2
B, S, D, E = 8, 512, 512, 1024
T = S // P
C = D // P
KE = E // P
UNITS = LAYERS * B
HEADS = (8, 16)
EPS = 1e-5
RING = 6
UP = 2.0**13
NORM_MAX = float(D) ** 0.5 * 1.001
MASK_ADD = 1e6
MASKED_OUT = -3e38
EXP_BITS = 0x7F800000
TINY = 2.0**-38

F32 = mybir.dt.float32
F16 = mybir.dt.float16
I32 = mybir.dt.int32
ALU = mybir.AluOpType
ACT = mybir.ActivationFunctionType
AX_X = mybir.AxisListType.X
RMAX = bass.bass_isa.ReduceOp.max

LN_W, LN_B, B_K, LN2_W, LN2_B, B_EMB = 0, 4, 8, 12, 16, 20
COLS = 28
LN = 7

STAGES = [("K", 0), ("YT", -1), ("V", 0), ("KT", 0), ("Q", 0), ("XT", 1), ("O", -1), ("QT", 0), ("Y", 0)]
OFFSET = dict(STAGES)
SLOTS = [(name, i) for name, _ in STAGES for i in range(4)]
assert len(SLOTS) % RING == 0


def order(u):
    if not isinstance(u, int):
        return SLOTS
    here = [(name, i) for name, i in SLOTS if 0 <= u + OFFSET[name] < UNITS]
    if u == UNITS - 1:
        here = [n for n in here if n[0] != "O"] + [("O", 0), ("O", 1), ("O", 2)]
    if u == UNITS:
        here = [n for n in here if n[0] == "YT"] + [("O'", 3)]
    return here


def slot(name, i):
    return SLOTS.index((name.rstrip("'"), i)) % RING


def previous_user(name, i, u):
    place, now = order(u).index((name, i)), u
    while True:
        if place == 0:
            now = now - 1
            if isinstance(now, int) and now < -1:
                return None
            place = len(order(now))
            continue
        place -= 1
        before, n = order(now)[place]
        if slot(before, n) == slot(name, i):
            return before.rstrip("'"), n, now + OFFSET[before.rstrip("'")] - (before == "O'")


def build(nc, x_d, emb_d, mask0_d, mask1_d, maskcol0_d, maskcol1_d, w_d, bias_d, wemb_d, cols_d, ident_d, blocks_d, out_d):
    with ExitStack() as ctx:
        def sb(name, shape, dt):
            return ctx.enter_context(nc.sbuf_tensor("sb_" + name, shape, dt))

        def sem(name):
            return ctx.enter_context(nc.semaphore(name))

        x = sb("x", [P, B * T, D], F32)
        w_hi = [sb(f"w_hi{i}", [P, C, D], F16) for i in range(5)]
        w_lo = [sb(f"w_lo{i}", [P, C, D], F16) for i in range(5)]
        w_stage = sb("w_stage", [P, C, D], F32)
        xh_or_h = sb("xh_or_h", [P, T, D], F32)
        k_or_qt = sb("k_or_qt", [P, C, S], F32)
        kt_or_y = sb("kt_or_y", [P, T, D], F32)
        v = sb("v", [P, T, D], F32)
        q = sb("q", [P, T, D], F32)
        xt_hi = sb("xt_hi", [P, C, S], F16)
        xt_lo = sb("xt_lo", [P, C, S], F16)
        ht_hi = sb("ht_hi", [P, C, S], F16)
        ht_lo = sb("ht_lo", [P, C, S], F16)
        att = sb("att", [P, C, P], F32)
        tanh = sb("tanh", [P, 2, S], F32)
        mask_raw = sb("mask_raw", [P, S], F32)
        mask_add = sb("mask_add", [P, S], F32)
        bias_q = [sb(f"bias_q{i}", [P, D], F32) for i in range(LAYERS)]
        bias_v = [sb(f"bias_v{i}", [P, D], F32) for i in range(LAYERS)]
        bias_o = [sb(f"bias_o{i}", [P, D], F32) for i in range(LAYERS)]
        wemb = sb("wemb", [P, 2, KE, P], F32)
        cols = sb("cols", [P, LAYERS, COLS], F32)
        ln_now = sb("ln_now", [P, LAYERS, 2, C], F32)
        ident = sb("ident", [P, P], F32)
        blocks = sb("blocks", [P, LAYERS, P], F32)
        film = [sb(f"film{i}", [P, B, 4, C], F32) for i in range(LAYERS)]
        film_now = sb("film_now", [P, 4, C], F32)
        mask_cols = sb("mask_cols", [P, LAYERS, B, T], F32)
        mask_int = sb("mask_int", [P, B, T], I32)
        mask_now = sb("mask_now", [P, T], F32)
        emb = sb("emb", [P, KE, B], F32)
        emb_half = sb("emb_half", [P, KE, B], F32)
        emb_tanh = sb("emb_tanh", [P, KE, B], F32)
        film_f = sb("film_f", [P, 2 * C, B], F32)
        film_g = sb("film_g", [P, C, B], F32)
        film_s = sb("film_s", [P, C, B], F32)
        peak = sb("peak", [P, LAYERS, 8], F32)
        peak_all = sb("peak_all", [P, LAYERS, 8], F32)
        scale_up = sb("scale_up", [P, LAYERS, 8], F32)
        scale_down = sb("scale_down", [P, LAYERS, 8], F32)
        down_o = sb("down_o", [P, LAYERS], F32)
        mask_scale = sb("mask_scale", [P, 1], F32)
        warm = sb("warm", [P, 1], F32)
        k_max = sb("k_max", [P, C], F32)
        k_top = sb("k_top", [P, C], F32)
        k_shift = sb("k_shift", [P, C], F32)
        k_sum = sb("k_sum", [P, C], F32)
        k_recip = sb("k_recip", [P, C], F32)
        q_max = sb("q_max", [P, T, max(HEADS)], F32)
        q_sum = sb("q_sum", [P, T, max(HEADS)], F32)
        q_recip = sb("q_recip", [P, T, max(HEADS)], F32)
        minus_half = sb("minus_half", [P, T], F32)
        x_stats = sb("x_stats", [P, T, 6], F32)
        x_mean_var = sb("x_mean_var", [P, T, 2], F32)
        x_var = sb("x_var", [P, T], F32)
        x_rstd = sb("x_rstd", [P, T], F32)
        x_add = sb("x_add", [P, T], F32)
        y_stats = sb("y_stats", [P, T, 6], F32)
        y_mean_var = sb("y_mean_var", [P, T, 2], F32)
        y_var = sb("y_var", [P, T], F32)
        y_rstd = sb("y_rstd", [P, T], F32)
        y_add = sb("y_add", [P, T], F32)
        spare = sb("spare", [P, 6], F32)
        ring = [ctx.enter_context(nc.psum_tensor(f"ring{i}", [P, 512], F32)) for i in range(RING)]
        att_ps = ctx.enter_context(nc.psum_tensor("att_ps", [P, C, P], F32))
        film_ps = ctx.enter_context(nc.psum_tensor("film_ps", [P, 512], F32))

        def bank(name, i):
            return ring[slot(name, i)][:]

        last_o = [att_ps[:].rearrange("p c n -> p (c n)"), film_ps[:], ring[slot("O", 2)][:], ring[slot("O", 3)][:]]

        def xu(b):
            return x[:, bass.ds(b * T, T), :] if not isinstance(b, int) else x[:, b * T:b * T + T, :]

        def xt(b, t):
            return x[:, bass.ds(b * T + t, 1), :].squeeze(1) if not isinstance(b, int) else x[:, b * T + t, :]

        def batch(unit, layer):
            return unit - layer * B

        last_ht_hi, last_ht_lo = xt_hi, xt_lo

        K_, V_, Q_, O_ = range(4)
        HELD = ((0, 1, 2, 3), (4, 0, 1, 2))
        w_stage2 = wemb.rearrange("p a b c -> p (a b c)").rearrange("p (c n) -> p c n", c=C)
        stages = ((w_stage, kt_or_y, v, w_stage), (w_stage, w_stage2, w_stage, w_stage))
        wemb0 = x[:, 4 * T:8 * T, :].rearrange("p (k h) d -> p k (h d)", k=KE)

        x0_loaded = [sem(f"x0_loaded{t}") for t in range(T)]
        x1_loaded, x_loaded = sem("x1_loaded"), sem("x_loaded")
        cols_loaded, ident_loaded, tables_loaded = sem("cols_loaded"), sem("ident_loaded"), sem("tables_loaded")
        row_bias_loaded = [sem(f"row_bias_loaded{i}") for i in range(LAYERS)]
        w_loaded = [sem(f"w_loaded{i}") for i in range(4)]
        wemb0_loaded = sem("wemb0_loaded")
        wemb_loaded = [sem(f"wemb_loaded{i}") for i in range(2)]
        mask_loaded = sem("mask_loaded")
        out_stored = sem("out_stored")
        done = {name: sem("pe_" + name) for name, _ in STAGES}
        att_summed = sem("att_summed")
        film_summed = sem("film_summed")
        k_masked, film_read, v_ready, kt_ready = sem("k_masked"), sem("film_read"), sem("v_ready"), sem("kt_ready")
        q_biased, xn_ready, x_new, qt_ready = sem("q_biased"), sem("xn_ready"), sem("x_new"), sem("qt_ready")
        y_ready = sem("y_ready")
        FREES = {"K": k_masked, "YT": film_read, "V": v_ready, "KT": kt_ready, "Q": q_biased, "XT": xn_ready,
                 "O": x_new, "QT": qt_ready, "Y": y_ready}
        att_ready, film_ps_read = sem("att_ready"), sem("film_ps_read")
        mask_ready, mask_now_ready, film_now_ready = sem("mask_ready"), sem("mask_now_ready"), sem("film_now_ready")
        k_normed = sem("k_normed")
        k_top_ready, k_shift_ready, k_exp, k_recip_ready = sem("k_top_ready"), sem("k_shift_ready"), sem("k_exp"), sem("k_recip_ready")
        q_max_ready, q_centred, q_exp, q_summed, q_recip_ready = (
            sem("q_max_ready"), sem("q_centred"), sem("q_exp"), sem("q_summed"), sem("q_recip_ready"))
        x_stats_ready, x_mv_ready, x_var_ready, x_rstd_ready, x_affine_ready = (
            sem("x_stats_ready"), sem("x_mv_ready"), sem("x_var_ready"), sem("x_rstd_ready"), sem("x_affine_ready"))
        y_stats_ready, y_mv_ready, y_var_ready, y_rstd_ready, y_affine_ready = (
            sem("y_stats_ready"), sem("y_mv_ready"), sem("y_var_ready"), sem("y_rstd_ready"), sem("y_affine_ready"))
        xh_ready, yh_ready = sem("xh_ready"), sem("yh_ready")
        xt_hi_ready, xt_lo_ready = sem("xt_hi_ready"), sem("xt_lo_ready")
        h_ready, ht_hi_ready, ht_lo_ready, x_biased = sem("h_ready"), sem("ht_hi_ready"), sem("ht_lo_ready"), sem("x_biased")
        w_peak, w_peak_all, w_scale_ready, w_hi_ready, w_ready = (
            sem("w_peak"), sem("w_peak_all"), sem("w_scale_ready"), sem("w_hi_ready"), sem("w_ready"))
        film_peak, film_peak_all = sem("film_peak"), sem("film_peak_all")
        ln_peak, ln_peak_all, ln_ready = sem("ln_peak"), sem("ln_peak_all"), sem("ln_ready")
        consts_ready, emb_tanh_ready, emb_ready = sem("consts_ready"), sem("emb_tanh_ready"), sem("emb_ready")
        dve_chain = sem("dve_chain")

        block = ctx.enter_context(nc.Block())

        @block.sync
        def _(sp):
            def load_mask(layer, b):
                src = (mask0_d, mask1_d)[layer]
                row = src[b:b + 1, :] if isinstance(b, int) else src[bass.ds(b, 1), :]
                dst = mask_raw[:] if layer == 0 else mask_raw[:].bitcast(I32)
                sp.dma_start(dst, row.broadcast_to([P, S])).then_inc(mask_loaded, 16)

            def load_w(layer, m):
                if (layer, m) == (0, O_):
                    sp.wait_ge(w_ready, 1)
                elif (layer, m) in ((1, K_), (1, O_)):
                    sp.wait_ge(w_ready, 4 * layer + m)
                elif (layer, m) == (1, Q_):
                    sp.wait_ge(w_ready, 4 + V_)
                sp.dma_start(stages[layer][m][:], w_d[layer][m].rearrange("(c p) n -> p c n", p=P)).then_inc(w_loaded[m], 16)

            def load_row_biases(layer):
                for dst, src in zip((bias_v, bias_q, bias_o), bias_d[layer]):
                    sp.dma_start(dst[layer][:], src.rearrange("(a d) -> a d", a=1).broadcast_to([P, D])).then_inc(
                        row_bias_loaded[layer], 16)

            def load_wemb1(js):
                for j in js:
                    if j == 0:
                        sp.wait_ge(w_ready, 4 + Q_)
                    if j >= 2:
                        sp.wait_ge(film_summed, 2 * C + j - 1)
                    sp.dma_start(wemb[:, j % 2], wemb_d[1].rearrange("(k p) n -> p k n", p=P)[:, :, j * P:j * P + P]
                                 ).then_inc(wemb_loaded[j % 2], 16)

            def step(u, back, following):
                if following is not None:
                    sp.wait_ge(mask_ready, u + 1)
                    load_mask(following, batch(u + 1, following))
                if back == 1:
                    sp.wait_ge(x_new, 4 * u)
                    store(batch(u - 1, 1))

            def store(b):
                dst = out_d[b] if isinstance(b, int) else out_d[bass.ds(b, 1)].squeeze(0)
                sp.dma_start(dst.rearrange("(t p) d -> p t d", p=P), xu(b)).then_inc(out_stored, 16)

            def load_x(b, loaded):
                sp.dma_start(xu(b), x_d[b].rearrange("(t p) d -> p t d", p=P)).then_inc(loaded, 16)

            for t in range(T):
                sp.dma_start(xt(0, t), x_d[0, t * P:t * P + P, :]).then_inc(x0_loaded[t], 16)
                if t == 1:
                    sp.dma_start(cols[:], cols_d).then_inc(cols_loaded, 16)
            sp.dma_start(ident[:], ident_d).then_inc(ident_loaded, 16)
            load_w(0, K_)
            sp.dma_start(blocks[:], blocks_d).then_inc(tables_loaded, 16)
            sp.dma_start(mask_cols[:, 0], maskcol0_d).then_inc(tables_loaded, 16)
            sp.dma_start(mask_int[:], maskcol1_d).then_inc(tables_loaded, 16)
            sp.dma_start(emb[:], emb_d).then_inc(tables_loaded, 16)
            load_w(0, V_)
            load_mask(0, 0)
            load_w(0, Q_)
            load_row_biases(0)
            load_x(1, x1_loaded)
            sp.dma_start(wemb0, wemb_d[0].rearrange("(k p) n -> p k n", p=P)).then_inc(wemb0_loaded, 16)
            load_w(0, O_)
            load_row_biases(1)
            for b in range(2, 4):
                load_x(b, x_loaded)
            step(0, None, 0)
            load_w(1, V_)
            sp.wait_ge(film_summed, 2 * C)
            for b in range(4, B):
                load_x(b, x_loaded)
            load_w(1, K_)
            with sp.Fori(1, B - 1) as u:
                step(u, 0, 0)
            step(B - 1, 0, 1)
            load_w(1, Q_)
            load_w(1, O_)
            step(B, 0, 1)
            load_wemb1(range(2 * C))
            with sp.Fori(B + 1, UNITS - 1) as u:
                step(u, 1, 1)
            step(UNITS - 1, 1, None)
            for t in range(T):
                sp.wait_ge(x_new, 4 * (UNITS - 1) + t + 1)
                sp.dma_start(out_d[B - 1, t * P:t * P + P, :], xt(B - 1, t)).then_inc(out_stored, 16)
            sp.wait_ge(out_stored, 16 * (B - 1 + T))

        @block.tensor
        def _(pe):
            def take_bank(name, i, u):
                before = previous_user(name, i, u)
                if before is not None:
                    stage, n, unit = before
                    pe.wait_ge(FREES[stage], 4 * unit + n + 1)
                return bank(name, i)

            def product(out, pairs):
                for n, (lhs, rhs) in enumerate(pairs):
                    last = nc.tensor.matmul(out, lhs, rhs, start=(n == 0), stop=(n == len(pairs) - 1))
                return last

            def split_pairs(lhs_hi, lhs_lo, rhs_hi, rhs_lo):
                return [p for c in range(C) for p in ((lhs_hi(c), rhs_hi(c)), (lhs_hi(c), rhs_lo(c)), (lhs_lo(c), rhs_hi(c)))]

            def nothing(i):
                pass

            def project_features(name, u, m, layer, between=nothing):
                hi, lo = w_hi[HELD[layer][m]], w_lo[HELD[layer][m]]
                for i in range(C):
                    f = slice(i * P, i * P + P)
                    out = take_bank(name, i, u)
                    product(out, split_pairs(lambda c: hi[:, c, f], lambda c: lo[:, c, f],
                                             lambda c: xt_hi[:, c, :], lambda c: xt_lo[:, c, :])).then_inc(done[name], 1)
                    between(i)

            def project_tokens(name, u, m, layer, a_hi, a_lo, tiles=range(T), between=nothing):
                hi, lo = w_hi[HELD[layer][m]], w_lo[HELD[layer][m]]
                for i in tiles:
                    s = slice(i * P, i * P + P)
                    out = take_bank(name, i, u)
                    product(out, split_pairs(lambda c: a_hi[:, c, s], lambda c: a_lo[:, c, s],
                                             lambda c: hi[:, c, :], lambda c: lo[:, c, :])).then_inc(done[name.rstrip("'")], 1)
                    between(i)

            def turn(name, i, u, source):
                out = take_bank(name, i, u)
                for j in range(4):
                    last = nc.tensor.transpose(out[:, j * P:j * P + P], source(i, j), ident[:])
                last.then_inc(done[name], 1)

            def turn_x(u):
                for i in range(C):
                    if i == 0:
                        pe.wait_ge(xh_ready, 4 * (u + 2))
                    turn("XT", i, u, lambda c, t: xh_or_h[:, t, c * P:c * P + P])

            def sum_film(layer, js):
                if js[0] == 0:
                    if layer == 0:
                        pe.wait_ge(emb_ready, 1)
                        pe.wait_ge(wemb0_loaded, 16)
                    else:
                        pe.wait_ge(film_ps_read, 1)
                for j in js:
                    if layer == 0:
                        w = wemb0[:, :, j * P:j * P + P]
                    else:
                        pe.wait_ge(wemb_loaded[j % 2], 16 * (j // 2 + 1))
                        w = wemb[:, j % 2]
                    product(film_ps[:, j * B:j * B + B], [(w[:, k, :], emb[:, k, :]) for k in range(KE)]
                            ).then_inc(film_summed, 1)

            def attend(u):
                for i in range(T):
                    pe.wait_ge(q_exp, 4 * u + i + 1)
                    turn("QT", i, u, lambda t, c: q[:, t, c * P:c * P + P])
                pe.wait_ge(att_ready, u + 1)
                for t in range(T):
                    pe.wait_ge(qt_ready, 4 * u + t + 1)
                    out = take_bank("Y", t, u)
                    for c in range(C):
                        last = nc.tensor.matmul(out[:, c * P:c * P + P], k_or_qt[:, t, c * P:c * P + P], att[:, c, :],
                                                start=True, stop=True)
                    last.then_inc(done["Y"], 1)

            def step(u, front, back, following, first=False):
                def film_after(n):
                    def between(i):
                        if front == 0 or n == 4:
                            sum_film(front, [n + i])
                        elif i % 2:
                            sum_film(1, [n + i // 2])
                    return between if first else nothing

                pe.wait_ge(xt_lo_ready, 4 * (u + 1))
                if first:
                    pe.wait_ge(w_ready, 4 * front + K_ + 1)
                project_features("K", u, K_, front)
                if back is not None:
                    pe.wait_ge(yh_ready, 4 * u)
                    for i in range(C):
                        turn("YT", i, u, lambda c, t: kt_or_y[:, t, c * P:c * P + P])
                if first:
                    pe.wait_ge(w_ready, 4 * front + V_ + 1)
                project_tokens("V", u, V_, front, xt_hi, xt_lo, between=film_after(0))
                if front == 0:
                    pe.wait_ge(k_exp, 4 * (u + 1))
                else:
                    pe.wait_ge(k_normed, 4 * (batch(u, 1) + 1))
                for i in range(T):
                    turn("KT", i, u, lambda t, c: k_or_qt[:, c, t * P:t * P + P])
                if first:
                    pe.wait_ge(w_ready, 4 * front + Q_ + 1)
                project_tokens("Q", u, Q_, front, xt_hi, xt_lo, between=film_after((4, 2)[front]))
                pe.wait_ge(kt_ready, 4 * (u + 1))
                pe.wait_ge(v_ready, 4 * (u + 1))
                if not isinstance(u, int) or u:
                    pe.wait_ge(att_ready, u)
                for c in range(C):
                    f = slice(c * P, c * P + P)
                    left, right = (kt_or_y, v) if front == 0 else (v, kt_or_y)
                    last = product(att_ps[:, c, :], [(left[:, t, f], right[:, t, f]) for t in range(T)])
                last.then_inc(att_summed, 1)
                if following is not None:
                    turn_x(u)
                else:
                    attend(u)
                if back is not None:
                    pe.wait_ge(ht_lo_ready, 4 * u)
                    pe.wait_ge(w_ready, 4 * back + O_ + 1)
                    project_tokens("O", u, O_, back, ht_hi, ht_lo, range(T if following is not None else T - 1),
                                   film_after(4))
                if following is not None:
                    attend(u)

            def last_step(u, layer):
                banks = [take_bank("YT", i, u) for i in range(C)]
                for t in range(T):
                    pe.wait_ge(yh_ready, 4 * (u - 1) + t + 1)
                    for i in range(C):
                        turned = nc.tensor.transpose(banks[i][:, t * P:t * P + P], kt_or_y[:, t, i * P:i * P + P], ident[:])
                        if t == T - 1:
                            turned.then_inc(done["YT"], 1)
                project_tokens("O'", u, O_, layer, ht_hi, ht_lo, (T - 1,))
                hi, lo = w_hi[HELD[layer][O_]], w_lo[HELD[layer][O_]]
                pe.wait_ge(att_ready, UNITS)
                pe.wait_ge(film_ps_read, LAYERS)
                pe.wait_ge(x_new, 4 * (UNITS - 2) + 3)
                for c in range(C):
                    pe.wait_ge(ht_hi_ready, 4 * (u - 1) + c + 1)
                    for i in range(T):
                        s = slice(i * P, i * P + P)
                        if c == 0 and i == T - 1:
                            pe.wait_ge(x_new, 4 * (UNITS - 1))
                        nc.tensor.matmul(last_o[i], last_ht_hi[:, c, s], hi[:, c, :], start=(c == 0), stop=False)
                        nc.tensor.matmul(last_o[i], last_ht_hi[:, c, s], lo[:, c, :], start=False, stop=False)
                    pe.wait_ge(ht_lo_ready, 4 * (u - 1) + c + 1)
                    for i in range(T):
                        s = slice(i * P, i * P + P)
                        last = nc.tensor.matmul(last_o[i], last_ht_lo[:, c, s], hi[:, c, :], start=False, stop=(c == C - 1))
                        if c == C - 1:
                            last.then_inc(done["O"], 1)

            pe.wait_ge(ident_loaded, 16)
            turn_x(-1)
            step(0, 0, None, 0, first=True)
            with pe.Fori(1, B - 1) as u:
                step(u, 0, 0, 0)
            step(B - 1, 0, 0, 1)
            step(B, 1, 0, 1, first=True)
            with pe.Fori(B + 1, UNITS - 1) as u:
                step(u, 1, 1, 1)
            step(UNITS - 1, 1, 1, None)
            last_step(UNITS, 1)

        @block.vector
        def _(dve):
            links = [0]

            def link(ins):
                links[0] += 1
                ins.then_inc(dve_chain, 1)
                dve.wait_ge(dve_chain, links[0])

            def wait_here(semaphore, value, word):
                dve.wait_ge(semaphore, value)
                nc.vector.memset(spare[:, word:word + 1], 0.0)

            def power(layer, n):
                at = (slice(None), layer, slice(n, n + 1))
                link(nc.vector.tensor_scalar(scale_down[at].bitcast(I32), peak_all[at].bitcast(I32), EXP_BITS, None, ALU.bitwise_and))
                link(nc.vector.tensor_scalar(scale_up[at].bitcast(I32), scale_down[at].bitcast(I32), EXP_BITS, None, ALU.bitwise_xor))

            def find_peak(layer, m):
                dve.wait_ge(w_loaded[m], 16 * (layer + 1))
                at = peak[:, layer, m:m + 1]
                link(nc.vector.tensor_reduce(at, stages[layer][m][:].rearrange("p c n -> p (c n)"), AX_X, ALU.max,
                                             apply_absolute_value=True))
                nc.vector.tensor_scalar(at, at, TINY, None, ALU.max).then_inc(w_peak, 1)

            def find_scale(layer, m):
                dve.wait_ge(w_peak_all, 4 * layer + m + 1)
                power(layer, m)
                up, down = scale_up[:, layer, m:m + 1], scale_down[:, layer, m:m + 1]
                nc.vector.tensor_scalar(up, up, UP, None, ALU.mult).then_inc(w_scale_ready, 1)
                if m == O_:
                    link(nc.vector.tensor_scalar(down, down, 0.5 / UP, None, ALU.mult))
                else:
                    link(nc.vector.tensor_scalar(down, down, 0.5 / UP, scale_down[:, layer, LN:LN + 1], ALU.mult, ALU.mult))
                if layer == 0 and m == K_:
                    dve.wait_ge(w_scale_ready, 1)
                    link(nc.vector.tensor_scalar(mask_scale[:], up, scale_up[:, layer, LN:LN + 1], MASK_ADD, ALU.mult, ALU.mult))

            def split_low(layer, m):
                for c in range(C):
                    dve.wait_ge(w_hi_ready, 4 * (4 * layer + m) + c + 1)
                    last = nc.vector.scalar_tensor_tensor(out=w_lo[HELD[layer][m]][:, c, :], in0=stages[layer][m][:, c, :],
                                                          scalar=scale_up[:, layer, m:m + 1], in1=w_hi[HELD[layer][m]][:, c, :],
                                                          op0=ALU.mult, op1=ALU.subtract)
                last.then_inc(w_ready, 1)

            def ln_peaks(layer):
                for n, at in ((4, LN_W), (5, LN_B)):
                    link(nc.vector.tensor_reduce(peak[:, layer, n:n + 1], cols[:, layer, at:at + C], AX_X, ALU.max,
                                                 apply_absolute_value=True))
                at = peak[:, layer, LN:LN + 1]
                link(nc.vector.scalar_tensor_tensor(out=at, in0=peak[:, layer, 4:5], scalar=NORM_MAX,
                                                    in1=peak[:, layer, 5:6], op0=ALU.mult, op1=ALU.add))
                nc.vector.tensor_scalar(at, at, TINY, None, ALU.max).then_inc(ln_peak, 1)

            def ln_scales(layer):
                dve.wait_ge(ln_peak_all, layer + 1)
                power(layer, LN)
                up, down = scale_up[:, layer, LN:LN + 1], scale_down[:, layer, LN:LN + 1]
                link(nc.vector.tensor_scalar(up, up, UP, None, ALU.mult))
                link(nc.vector.tensor_scalar(down, down, 0.5 / UP, None, ALU.mult))
                nc.vector.tensor_scalar(ln_now[:, layer, 0, :], cols[:, layer, LN_W:LN_W + C], up, None, ALU.mult).then_inc(ln_ready, 1)
                nc.vector.tensor_scalar(ln_now[:, layer, 1, :], cols[:, layer, LN_B:LN_B + C], up, None, ALU.mult).then_inc(ln_ready, 1)

            def prepare_film(layer):
                wide = lambda at: cols[:, layer, at:at + C].unsqueeze(2).broadcast_to([P, C, B])
                dve.wait_ge(film_summed, 2 * C * (layer + 1))
                ins = nc.vector.tensor_tensor(film_f[:], film_ps[:, 0:2 * C * B].rearrange("p (j b) -> p j b", b=B),
                                              cols[:, layer, B_EMB:B_EMB + 2 * C].unsqueeze(2).broadcast_to([P, 2 * C, B]), ALU.add)
                ins.then_inc(film_ps_read, 1)
                dve.wait_ge(film_ps_read, layer + 1)
                link(nc.vector.tensor_scalar(film_f[:, 0:C, :], film_f[:, 0:C, :], 1.0, None, ALU.add))
                link(nc.vector.tensor_tensor(film_g[:], film_f[:, 0:C, :], wide(LN2_W), ALU.mult))
                link(nc.vector.tensor_tensor(film_s[:], film_f[:, 0:C, :], wide(LN2_B), ALU.mult))
                link(nc.vector.tensor_tensor(film_s[:], film_s[:], film_f[:, C:2 * C, :], ALU.add))
                link(nc.vector.tensor_reduce(peak[:, layer, 4:5], film_g[:].rearrange("p c b -> p (c b)"), AX_X, ALU.max,
                                             apply_absolute_value=True))
                link(nc.vector.tensor_reduce(peak[:, layer, 5:6], film_s[:].rearrange("p c b -> p (c b)"), AX_X, ALU.max,
                                             apply_absolute_value=True))
                link(nc.vector.scalar_tensor_tensor(out=peak[:, layer, 6:7], in0=peak[:, layer, 4:5], scalar=NORM_MAX,
                                                    in1=peak[:, layer, 5:6], op0=ALU.mult, op1=ALU.add))
                nc.vector.tensor_scalar(peak[:, layer, 6:7], peak[:, layer, 6:7], TINY, None, ALU.max).then_inc(film_peak, 1)
                dve.wait_ge(film_peak_all, layer + 1)
                power(layer, 6)
                link(nc.vector.tensor_scalar(scale_up[:, layer, 6:7], scale_up[:, layer, 6:7], UP, None, ALU.mult))
                link(nc.vector.tensor_scalar(scale_down[:, layer, 6:7], scale_down[:, layer, 6:7], 0.5 / UP, None, ALU.mult))
                table = lambda kind: film[layer][:, :, kind, :].rearrange("p b c -> p c b")
                up = scale_up[:, layer, 6:7]
                link(nc.vector.tensor_scalar(table(0), film_g[:], 0.5, None, ALU.mult))
                link(nc.vector.tensor_scalar(table(1), film_s[:], 0.5, None, ALU.mult))
                link(nc.vector.tensor_scalar(table(2), film_g[:], 0.5, up, ALU.mult, ALU.mult))
                link(nc.vector.tensor_scalar(table(3), film_s[:], 0.5, up, ALU.mult, ALU.mult))
                link(nc.vector.tensor_tensor(down_o[:, layer:layer + 1], scale_down[:, layer, O_:O_ + 1],
                                             scale_down[:, layer, 6:7], ALU.mult))

            def x_statistics(unit, layer):
                b = batch(unit, layer)
                if layer == 1:
                    dve.wait_ge(x_new, 4 * (b + 1))
                for t in range(T):
                    if isinstance(unit, int) and unit == 0:
                        dve.wait_ge(x0_loaded[t], 16)
                    nc.vector.bn_stats(x_stats[:, t, :], xt(b, t)).then_inc(x_stats_ready, 1)
                wait_here(x_stats_ready, 4 * (unit + 1), 4)
                for t in range(T):
                    nc.vector.bn_aggr(x_mean_var[:, t, :], x_stats[:, t, :]).then_inc(x_mv_ready, 1)
                dve.wait_ge(x_mv_ready, 4 * (unit + 1))
                nc.vector.tensor_scalar(x_var[:], x_mean_var[:, :, 1], EPS, None, ALU.add).then_inc(x_var_ready, 1)

            def x_affine(unit):
                dve.wait_ge(x_rstd_ready, unit + 1)
                nc.vector.scalar_tensor_tensor(out=x_add[:], in0=x_mean_var[:, :, 0], scalar=-1.0, in1=x_rstd[:],
                                               op0=ALU.mult, op1=ALU.mult).then_inc(x_affine_ready, 1)

            def step(u, front, back, following, prep=None):
                u_is_first = isinstance(u, int) and u == 0

                def residual(tiles, unit):
                    dve.wait_ge(x_biased, unit + 1)
                    b = batch(unit, back)
                    for t in tiles:
                        dve.wait_ge(done["O"], 4 * unit + t + 1)
                        nc.vector.scalar_tensor_tensor(out=xt(b, t), in0=bank("O", t) if not isinstance(unit, int) or unit < UNITS - 1 else last_o[t], scalar=down_o[:, back:back + 1],
                                                       in1=xt(b, t), op0=ALU.mult, op1=ALU.add).then_inc(x_new, 1)

                if back is not None:
                    dve.wait_ge(y_rstd_ready, u)
                    nc.vector.scalar_tensor_tensor(out=y_add[:], in0=y_mean_var[:, :, 0], scalar=-1.0, in1=y_rstd[:],
                                                   op0=ALU.mult, op1=ALU.mult).then_inc(y_affine_ready, 1)
                    b = batch(u - 1, back)
                    src = film[back][:, b] if isinstance(b, int) else film[back][:, bass.ds(b, 1)].squeeze(1)
                    nc.vector.tensor_copy(film_now[:], src).then_inc(film_now_ready, 1)
                if front is None:
                    residual(range(T - 1), u - 2)
                if front is not None:
                    heads = HEADS[front]
                    dve.wait_ge(mask_loaded, 16 * (u + 1))
                    if front == 0:
                        nc.vector.tensor_scalar(mask_add[:], mask_raw[:], 1.0, mask_scale[:], ALU.subtract, ALU.mult
                                                ).then_inc(mask_ready, 1)
                    else:
                        nc.vector.tensor_scalar(mask_add[:], mask_raw[:].bitcast(I32), 1.0, MASKED_OUT, ALU.is_equal, ALU.mult
                                                ).then_inc(mask_ready, 1)
                    b = batch(u, front)
                    src = mask_cols[:, front, b] if isinstance(b, int) else mask_cols[:, front, bass.ds(b, 1)].squeeze(1)
                    nc.vector.tensor_copy(mask_now[:], src).then_inc(mask_now_ready, 1)
                    dve.wait_ge(mask_ready, u + 1)
                    for i in range(C):
                        wait_here(done["K"], 4 * u + i + 1, i)
                        nc.vector.tensor_tensor_reduce(k_or_qt[:, i, :], bank("K", i), mask_add[:],
                                                       scale_down[:, front, K_:K_ + 1], -3.4e38, ALU.add, ALU.max,
                                                       k_max[:, i:i + 1]).then_inc(k_masked, 1)
                    bias_k = cols[:, front, B_K:B_K + C]
                    dve.wait_ge(k_masked, 4 * (u + 1))
                    nc.vector.tensor_tensor(k_top[:], k_max[:], bias_k, ALU.add).then_inc(k_top_ready, 1)
                    dve.wait_ge(k_top_ready, u + 1)
                    nc.vector.tensor_tensor(k_shift[:], bias_k, k_top[:], ALU.subtract).then_inc(k_shift_ready, 1)
                if prep == 1:
                    find_peak(1, K_)
                if following is not None:
                    x_statistics(u + 1, following)
                if prep == 1:
                    find_scale(1, K_)
                if u_is_first:
                    ln_peaks(1)
                if front is not None:
                    dve.wait_ge(k_exp, 4 * (u + 1))
                    nc.vector.reciprocal(k_recip[:], k_sum[:]).then_inc(k_recip_ready, 1)
                    dve.wait_ge(k_recip_ready, u + 1)
                    if front == 1:
                        for i in range(C):
                            nc.vector.tensor_scalar(k_or_qt[:, i, :], k_or_qt[:, i, :], k_recip[:, i:i + 1], None, ALU.mult
                                                    ).then_inc(k_normed, 1)
                if back is not None:
                    for c in range(C):
                        if front is None:
                            dve.wait_ge(film_read, 4 * (u - 1) + c + 1)
                            link(nc.vector.tensor_scalar(xh_or_h[:, c, :], bank("YT", c), film_now[:, 2, c:c + 1],
                                                         film_now[:, 3, c:c + 1], ALU.mult, ALU.add))
                            if c == 1:
                                residual((T - 1,), u - 2)
                        else:
                            dve.wait_ge(film_read, 4 * (u - 1) + c + 1)
                        nc.vector.scalar_tensor_tensor(out=xh_or_h[:, c, :], in0=tanh[:, c % 2, :], scalar=1.0,
                                                       in1=xh_or_h[:, c, :], op0=ALU.add, op1=ALU.mult).then_inc(h_ready, 1)
                    if front is None:
                        residual(range(T), u - 1)
                if u_is_first:
                    split_low(0, Q_)
                    ln_scales(1)
                if front is not None:
                    for t in range(T):
                        dve.wait_ge(done["V"], 4 * u + t + 1)
                        nc.vector.scalar_tensor_tensor(out=v[:, t, :], in0=bank("V", t), scalar=scale_down[:, front, V_:V_ + 1],
                                                       in1=bias_v[front][:], op0=ALU.mult, op1=ALU.add).then_inc(v_ready, 1)
                if prep == 1:
                    split_low(1, K_)
                if prep:
                    find_peak(1, V_ if prep == 1 else O_)
                if u_is_first:
                    find_peak(0, O_)
                if following is not None:
                    x_affine(u + 1)
                if prep:
                    find_scale(1, V_ if prep == 1 else O_)
                if u_is_first:
                    find_scale(0, O_)
                if front is not None:
                    by_head = lambda a: a.rearrange("p (h e) -> p h e", h=heads)
                    wide = lambda a: a.unsqueeze(2).broadcast_to([P, heads, D // heads])
                    for t in range(T):
                        dve.wait_ge(done["Q"], 4 * u + t + 1)
                        nc.vector.scalar_tensor_tensor(out=q[:, t, :], in0=bank("Q", t), scalar=scale_down[:, front, Q_:Q_ + 1],
                                                       in1=bias_q[front][:], op0=ALU.mult, op1=ALU.add).then_inc(q_biased, 1)
                        dve.wait_ge(q_biased, 4 * u + t + 1)
                        nc.vector.tensor_reduce(q_max[:, t, 0:heads], by_head(q[:, t, :]), AX_X, ALU.max).then_inc(q_max_ready, 1)
                        dve.wait_ge(q_max_ready, 4 * u + t + 1)
                        nc.vector.tensor_tensor(by_head(q[:, t, :]), by_head(q[:, t, :]), wide(q_max[:, t, 0:heads]),
                                                ALU.subtract).then_inc(q_centred, 1)
                    dve.wait_ge(att_summed, u + 1)
                    if front == 0:
                        for c in range(C):
                            last = nc.vector.scalar_tensor_tensor(out=att[:, c, :], in0=att_ps[:, c, :],
                                                                  scalar=k_recip[:, c:c + 1], in1=blocks[:, 0, :],
                                                                  op0=ALU.mult, op1=ALU.mult)
                    else:
                        last = nc.vector.tensor_tensor(att[:], att_ps[:], blocks[:, 1:2, :].broadcast_to([P, C, P]), ALU.mult)
                    last.then_inc(att_ready, 1)
                if front is not None:
                    for t in range(T):
                        dve.wait_ge(q_exp, 4 * u + t + 1)
                        nc.vector.tensor_reduce(q_sum[:, t, 0:heads], by_head(q[:, t, :]), AX_X, ALU.add).then_inc(q_summed, 1)
                    dve.wait_ge(q_summed, 4 * (u + 1))
                    nc.vector.reciprocal(q_recip[:, :, 0:heads], q_sum[:, :, 0:heads]).then_inc(q_recip_ready, 1)
                if prep == 1:
                    find_peak(1, Q_)

                if back is not None and following is not None:
                    residual(range(2), u - 1)
                if prep:
                    split_low(1, V_ if prep == 1 else O_)
                if back is not None and following is not None:
                    residual(range(2, T), u - 1)
                if prep == 1:
                    find_scale(1, Q_)
                if u_is_first:
                    prepare_film(0)
                if front is not None:
                    dve.wait_ge(q_recip_ready, u + 1)
                    for t in range(T + 1):
                        if t < T:
                            dve.wait_ge(done["Y"], 4 * u + t + 1)
                            nc.vector.tensor_tensor(by_head(kt_or_y[:, t, :]), by_head(bank("Y", t)),
                                                    wide(q_recip[:, t, 0:heads]), ALU.mult).then_inc(y_ready, 1)
                        if t:
                            dve.wait_ge(y_ready, 4 * u + t)
                            nc.vector.bn_stats(y_stats[:, t - 1, :], kt_or_y[:, t - 1, :]).then_inc(y_stats_ready, 1)
                    wait_here(y_stats_ready, 4 * (u + 1), 5)
                    for t in range(T):
                        nc.vector.bn_aggr(y_mean_var[:, t, :], y_stats[:, t, :]).then_inc(y_mv_ready, 1)
                    dve.wait_ge(y_mv_ready, 4 * (u + 1))
                    nc.vector.tensor_scalar(y_var[:], y_mean_var[:, :, 1], EPS, None, ALU.add).then_inc(y_var_ready, 1)
                if u_is_first:
                    split_low(0, O_)
                if prep == 1:
                    split_low(1, Q_)

            nc.vector.memset(minus_half[:], -0.5).then_inc(consts_ready, 1)
            x_statistics(0, 0)
            dve.wait_ge(cols_loaded, 16)
            ln_peaks(0)
            x_affine(0)
            ln_scales(0)
            find_peak(0, K_)
            dve.wait_ge(tables_loaded, 64)
            link(nc.vector.tensor_scalar(mask_cols[:, 1], mask_int[:], 1.0, None, ALU.not_equal))
            link(nc.vector.tensor_scalar(emb_half[:], emb[:], 0.5, None, ALU.mult))
            find_scale(0, K_)
            split_low(0, K_)
            find_peak(0, V_)
            for c in range(C):
                dve.wait_ge(xt_hi_ready, c + 1)
                nc.vector.tensor_tensor(xt_lo[:, c, :], xh_or_h[:, c, :], xt_hi[:, c, :], ALU.subtract).then_inc(xt_lo_ready, 1)
            find_scale(0, V_)
            find_peak(0, Q_)
            split_low(0, V_)
            find_scale(0, Q_)
            dve.wait_ge(emb_tanh_ready, 1)
            nc.vector.scalar_tensor_tensor(out=emb[:], in0=emb_tanh[:], scalar=1.0, in1=emb_half[:], op0=ALU.add, op1=ALU.mult
                                           ).then_inc(emb_ready, 1)
            dve.wait_ge(row_bias_loaded[0], 48)
            dve.wait_ge(x1_loaded, 16)
            step(0, 0, None, 0)
            dve.wait_ge(row_bias_loaded[1], 48)
            dve.wait_ge(x_loaded, 16 * (B - 2))
            with dve.Fori(1, B - 1) as u:
                step(u, 0, 0, 0)
            step(B - 1, 0, 0, 1, prep=1)
            step(B, 1, 0, 1, prep=2)
            prepare_film(1)
            with dve.Fori(B + 1, UNITS - 1) as u:
                step(u, 1, 1, 1)
            step(UNITS - 1, 1, 1, None)
            step(UNITS, None, 1, None)

        @block.scalar
        def _(act):
            def split_high(layer, m):
                act.wait_ge(w_scale_ready, 4 * layer + m + 1)
                if layer == 1 and m != K_:
                    act.wait_ge(done[("K", "V", "Q")[HELD[1][m]]], 4 * B)
                for c in range(C):
                    nc.scalar.activation(w_hi[HELD[layer][m]][:, c, :], stages[layer][m][:, c, :], ACT.Copy,
                                         scale=scale_up[:, layer, m:m + 1]).then_inc(w_hi_ready, 1)

            def normalise_x(unit, layer, after_h):
                b = batch(unit, layer)
                act.wait_ge(x_affine_ready, unit + 1)
                if after_h is not None:
                    act.wait_ge(ht_lo_ready, 4 * after_h)
                elif unit:
                    act.wait_ge(xt_lo_ready, 4 * unit)
                for t in range(T):
                    nc.scalar.activation(xh_or_h[:, t, :], xt(b, t), ACT.Identity, bias=x_add[:, t:t + 1],
                                         scale=x_rstd[:, t:t + 1]).then_inc(xh_ready, 1)

            def turned_x(unit, layer):
                act.wait_ge(done["XT"], 4 * (unit + 1))
                for c in range(C):
                    nc.scalar.activation(xh_or_h[:, c, :], bank("XT", c), ACT.Identity, bias=ln_now[:, layer, 1, c:c + 1],
                                         scale=ln_now[:, layer, 0, c:c + 1]).then_inc(xn_ready, 1)
                for c in range(C):
                    act.wait_ge(xn_ready, 4 * unit + c + 1)
                    nc.scalar.copy(xt_hi[:, c, :], xh_or_h[:, c, :]).then_inc(xt_hi_ready, 1)

            def step(u, front, back, following, prep=None):
                def high(c):
                    act.wait_ge(h_ready, 4 * (u - 1) + c + 1)
                    nc.scalar.copy((ht_hi if front is not None else last_ht_hi)[:, c, :], xh_or_h[:, c, :]).then_inc(ht_hi_ready, 1)

                if back is not None:
                    act.wait_ge(y_affine_ready, u)
                    for t in range(T):
                        nc.scalar.activation(kt_or_y[:, t, :], kt_or_y[:, t, :], ACT.Identity, bias=y_add[:, t:t + 1],
                                             scale=y_rstd[:, t:t + 1]).then_inc(yh_ready, 1)
                if front is not None:
                    act.wait_ge(k_shift_ready, u + 1)
                    for i in range(C):
                        nc.scalar.activation(k_or_qt[:, i, :], k_or_qt[:, i, :], ACT.Exp, bias=k_shift[:, i:i + 1],
                                             accum_out=k_sum[:, i:i + 1]).then_inc(k_exp, 1)
                if back is not None:
                    act.wait_ge(film_now_ready, u)
                    for c in range(C):
                        act.wait_ge(done["YT"], 4 * (u - 1) + c + 1)
                        if c >= 2:
                            act.wait_ge(h_ready, 4 * (u - 1) + c - 1)
                        turned = nc.scalar.activation(tanh[:, c % 2, :], bank("YT", c), ACT.Tanh, bias=film_now[:, 1, c:c + 1],
                                                      scale=film_now[:, 0, c:c + 1])
                        if front is None:
                            turned.then_inc(film_read, 1)
                            if c:
                                high(c - 1)
                            continue
                        nc.scalar.activation(xh_or_h[:, c, :], bank("YT", c), ACT.Identity, bias=film_now[:, 3, c:c + 1],
                                             scale=film_now[:, 2, c:c + 1]).then_inc(film_read, 1)
                    for c in range(C) if front is not None else (C - 1,):
                        high(c)
                if prep == 1:
                    split_high(1, K_)
                if front is not None:
                    act.wait_ge(mask_now_ready, u + 1)
                    for t in range(T):
                        act.wait_ge(done["KT"], 4 * u + t + 1)
                        nc.scalar.activation(kt_or_y[:, t, :], bank("KT", t), ACT.Copy, scale=mask_now[:, t:t + 1]
                                             ).then_inc(kt_ready, 1)
                if following is not None:
                    normalise_x(u + 1, following, u if back is not None else None)
                if front is not None:
                    for t in range(T):
                        act.wait_ge(q_centred, 4 * u + t + 1)
                        nc.scalar.activation(q[:, t, :], q[:, t, :], ACT.Exp).then_inc(q_exp, 1)
                if following is not None:
                    turned_x(u + 1, following)
                if isinstance(u, int) and u == 0:
                    split_high(0, O_)
                if prep:
                    split_high(1, V_ if prep == 1 else O_)
                if front is not None:
                    for t in range(T):
                        act.wait_ge(done["QT"], 4 * u + t + 1)
                        nc.scalar.copy(k_or_qt[:, t, :], bank("QT", t)).then_inc(qt_ready, 1)
                if prep == 1:
                    split_high(1, Q_)

            act.wait_ge(consts_ready, 1)
            nc.scalar.activation(warm[:], minus_half[:, 0:1], ACT.Tanh)
            normalise_x(0, 0, None)
            split_high(0, K_)
            act.wait_ge(ln_ready, 2)
            turned_x(0, 0)
            act.wait_ge(tables_loaded, 64)
            nc.scalar.activation(emb_tanh[:], emb[:], ACT.Tanh, scale=0.5).then_inc(emb_tanh_ready, 1)
            split_high(0, V_)
            split_high(0, Q_)
            step(0, 0, None, 0)
            with act.Fori(1, B - 1) as u:
                step(u, 0, 0, 0)
            act.wait_ge(ln_ready, 4)
            step(B - 1, 0, 0, 1, prep=1)
            step(B, 1, 0, 1, prep=2)
            with act.Fori(B + 1, UNITS - 1) as u:
                step(u, 1, 1, 1)
            step(UNITS - 1, 1, 1, None)
            step(UNITS, None, 1, None)

        @block.gpsimd
        def _(pool):
            def x_power(unit):
                pool.wait_ge(x_var_ready, unit + 1)
                nc.gpsimd.tensor_tensor(x_rstd[:], x_var[:], minus_half[:], ALU.pow).then_inc(x_rstd_ready, 1)

            def x_low_part(unit):
                for c in range(C):
                    pool.wait_ge(xt_hi_ready, 4 * unit + c + 1)
                    nc.gpsimd.tensor_tensor(xt_lo[:, c, :], xh_or_h[:, c, :], xt_hi[:, c, :], ALU.subtract).then_inc(xt_lo_ready, 1)

            def add_bias(unit, layer):
                b = batch(unit, layer)
                pool.wait_ge(xh_ready, 4 * (unit + 1))
                nc.gpsimd.tensor_tensor(xu(b), xu(b), bias_o[layer][:].unsqueeze(1).broadcast_to([P, T, D]), ALU.add
                                        ).then_inc(x_biased, 1)

            def prepare_w(layer, m):
                pool.wait_ge(w_peak, 4 * layer + m + 1)
                nc.gpsimd.partition_all_reduce(peak_all[:, layer, m:m + 1], peak[:, layer, m:m + 1], P, RMAX).then_inc(w_peak_all, 1)

            def prepare_ln(layer):
                pool.wait_ge(ln_peak, layer + 1)
                nc.gpsimd.partition_all_reduce(peak_all[:, layer, LN:LN + 1], peak[:, layer, LN:LN + 1], P, RMAX).then_inc(ln_peak_all, 1)

            def prepare_film(layer):
                pool.wait_ge(film_peak, layer + 1)
                nc.gpsimd.partition_all_reduce(peak_all[:, layer, 6:7], peak[:, layer, 6:7], P, RMAX).then_inc(film_peak_all, 1)

            def step(u, front, back, following, prep=None):
                if back is not None:
                    pool.wait_ge(y_var_ready, u)
                    nc.gpsimd.tensor_tensor(y_rstd[:], y_var[:], minus_half[:], ALU.pow).then_inc(y_rstd_ready, 1)
                if prep == 1:
                    prepare_w(1, K_)
                if following is not None:
                    x_power(u + 1)
                if back is not None:
                    hi, lo = (ht_hi, ht_lo) if front is not None else (last_ht_hi, last_ht_lo)
                    for c in range(C):
                        pool.wait_ge(ht_hi_ready, 4 * (u - 1) + c + 1)
                        nc.gpsimd.tensor_tensor(lo[:, c, :], xh_or_h[:, c, :], hi[:, c, :], ALU.subtract
                                                ).then_inc(ht_lo_ready, 1)
                if prep:
                    prepare_w(1, V_ if prep == 1 else O_)
                if following is not None:
                    add_bias(u + 1, following)
                    x_low_part(u + 1)
                if prep == 1:
                    prepare_w(1, Q_)

            pool.wait_ge(consts_ready, 1)
            x_power(0)
            prepare_ln(0)
            prepare_w(0, K_)
            prepare_w(0, V_)
            prepare_w(0, Q_)
            x_power(1)
            pool.wait_ge(row_bias_loaded[0], 48)
            add_bias(0, 0)
            prepare_ln(1)
            prepare_w(0, O_)
            add_bias(1, 0)
            prepare_film(0)
            x_low_part(1)
            with pool.Fori(1, B - 1) as u:
                step(u, 0, 0, 0)
            pool.wait_ge(row_bias_loaded[1], 48)
            step(B - 1, 0, 0, 1, prep=1)
            step(B, 1, 0, 1, prep=2)
            prepare_film(1)
            with pool.Fori(B + 1, UNITS - 1) as u:
                step(u, 1, 1, 1)
            step(UNITS - 1, 1, 1, None)
            step(UNITS, None, 1, None)


_W = (("L0_cond_Wk", "L0_cond_Wv", "L0_cond_Wq", "L0_cond_W_out"),
      ("L1_cond_Wk", "L1_cond_Wv", "L1_cond_Wq", "L1_cond_film_out_W"))
_ROWS = (("L0_cond_bv", "L0_cond_bq", "L0_cond_b_out"),
         ("L1_cond_bv", "L1_cond_bq", "L1_cond_film_out_b"))
_WEMB = ("L0_cond_W_emb", "L1_cond_film_emb_W")
_COLS = (("L0_cond_ln_w", "L0_cond_ln_b", "L0_cond_bk", "L0_cond_ln2_w", "L0_cond_ln2_b", "L0_cond_b_emb"),
         ("L1_cond_norm_scale", "L1_cond_norm_bias", "L1_cond_bk", "L1_cond_film_norm_scale",
          "L1_cond_film_norm_bias", "L1_cond_film_emb_b"))


def kernel(**inputs):
    import numpy as np
    import concourse.bacc as bacc
    from concourse.bass_utils import run_bass_kernel_spmd

    a = {k: np.ascontiguousarray(v) for k, v in inputs.items()}

    def by_partition(rows, n):
        rows = rows.reshape(*rows.shape[:-1], n, P)
        return np.ascontiguousarray(np.moveaxis(rows, -1, 0))

    mask0 = a["mask_BxSx1_fk1"].reshape(B, S)
    mask1 = a["mask_BxS_ik0"].reshape(B, S)
    arrays = {
        "x": a["x"], "mask0": mask0, "mask1": mask1,
        "emb": np.ascontiguousarray(by_partition(a["cond_2048"], KE).transpose(0, 2, 1)),
        "maskcol0": by_partition(mask0, T), "maskcol1": by_partition(mask1, T),
        "cols": np.stack([np.concatenate([by_partition(a[n], a[n].size // P) for n in names], 1) for names in _COLS], 1),
        "ident": np.eye(P, dtype=np.float32),
        "blocks": np.stack([np.kron(np.eye(P * h // D), np.ones((D // h, D // h))) for h in HEADS], 1).astype(np.float32),
    }
    for names in (*_W, *_ROWS, _WEMB):
        for n in names:
            arrays[n] = a[n]
    nc = bacc.Bacc("TRN2", target_bir_lowering=False, num_devices=1)
    arrays = {f"in_{k}": np.ascontiguousarray(v) for k, v in arrays.items()}
    ap = {k[3:]: nc.dram_tensor(k, v.shape, mybir.dt.from_np(v.dtype), kind="ExternalInput").ap() for k, v in arrays.items()}
    out = nc.dram_tensor("out_0", (B, S, D), F32, kind="ExternalOutput").ap()
    build(nc, ap["x"], ap["emb"], ap["mask0"], ap["mask1"], ap["maskcol0"], ap["maskcol1"],
          [[ap[n] for n in names] for names in _W], [[ap[n] for n in names] for names in _ROWS],
          [ap[n] for n in _WEMB], ap["cols"], ap["ident"], ap["blocks"], out)
    r = run_bass_kernel_spmd(nc, [arrays], core_ids=[0])
    return r.results[0]["out_0"]
```

```python
from contextlib import ExitStack

import concourse.bass as bass
from concourse import mybir

P = 128
LAYERS = 2
B, S, D, E = 8, 512, 512, 1024
T = S // P
C = D // P
KE = E // P
UNITS = LAYERS * B
HEADS = (8, 16)
EPS = 1e-5
RING = 6
UP = 2.0**13
NORM_MAX = float(D) ** 0.5 * 1.001
ONE = 2.0**15
MASK_ADD = 1e6
MASKED_OUT = -3e38
EXP_BITS = 0x7F800000
TINY = 2.0**-38

F32 = mybir.dt.float32
F16 = mybir.dt.float16
I32 = mybir.dt.int32
ALU = mybir.AluOpType
ACT = mybir.ActivationFunctionType
AX_X = mybir.AxisListType.X
RMAX = bass.bass_isa.ReduceOp.max

LN_W, LN_B, B_K, LN2_W, LN2_B, B_EMB = 0, 4, 8, 12, 16, 20
COLS = 28
LN, V_BOUND = 7, 4

STAGES = [("K", 0), ("YT", -1), ("V", 0), ("Q", 0), ("XT", 1), ("O", -1), ("Y", 0)]
OFFSET = dict(STAGES)
SLOTS = [(name, i) for name, _ in STAGES for i in range(4)]


def order(u):
    if not isinstance(u, int):
        return SLOTS
    here = [(name, i) for name, i in SLOTS if 0 <= u + OFFSET[name] < UNITS]
    if u == UNITS - 1:
        y = here.index(("Y", 0))
        here = [n for n in here[:y] if n != ("O", 3)] + here[y:]
    if u == UNITS:
        here = [n for n in here if n[0] == "YT"] + [("O'", 3)]
    return here


def slot(name, i):
    return 3 if name == "O'" else slot("O", i) if name == "Y" else SLOTS.index((name, i)) % RING


def previous_user(name, i, u):
    place, now = order(u).index((name, i)), u
    while True:
        if place == 0:
            now = now - 1
            if isinstance(now, int) and now < -1:
                return None
            place = len(order(now))
            continue
        place -= 1
        before, n = order(now)[place]
        if slot(before, n) == slot(name, i):
            return before.rstrip("'"), n, now + OFFSET[before.rstrip("'")] - (before == "O'")


def build(nc, x_d, emb_d, mask0_d, mask1_d, w_d, bias_d, wemb_d, cols_d, ident_d, blocks_d, out_d):
    with ExitStack() as ctx:
        def sb(name, shape, dt):
            return ctx.enter_context(nc.sbuf_tensor("sb_" + name, shape, dt))

        def sem(name):
            return ctx.enter_context(nc.semaphore(name))

        x = sb("x", [P, B * T, D], F32)
        w_hi = [sb(f"w_hi{i}", [P, C, D], F16) for i in range(5)]
        w_lo = [sb(f"w_lo{i}", [P, C, D], F16) for i in range(5)]
        w_stage = sb("w_stage", [P, C, D], F32)
        xh_or_h = sb("xh_or_h", [P, T, D], F32)
        k_or_qt = sb("k_or_qt", [P, C, S], F32)
        kt_or_y = sb("kt_or_y", [P, T, D], F32)
        v_parts = sb("v_parts", [P, T, D], F32)
        v_or_q = sb("v_or_q", [P, T, D], F32)
        kq_hi = sb("kq_hi", [P, C * S], F16)
        xt_hi = sb("xt_hi", [P, C, S], F16)
        xt_lo = sb("xt_lo", [P, C, S], F16)
        ht_hi = sb("ht_hi", [P, C, S], F16)
        ht_lo = sb("ht_lo", [P, C, S], F16)
        att = sb("att", [P, C, P], F32)
        att_hi = sb("att_hi", [P, C, P], F16)
        att_lo = sb("att_lo", [P, C, P], F16)
        tanh = sb("tanh", [P, 2, S], F32)
        mask_raw = sb("mask_raw", [P, S], F32)
        mask_add = sb("mask_add", [P, S], F32)
        bias_q = sb("bias_q", [P, D], F32)
        bias_v = [sb(f"bias_v{i}", [P, D], F32) for i in range(LAYERS)]
        bias_o = sb("bias_o", [P, D], F32)
        wemb = sb("wemb", [P, 2, KE, P], F32)
        cols = sb("cols", [P, LAYERS, COLS], F32)
        ln_now = sb("ln_now", [P, LAYERS, 2, C], F32)
        ident = sb("ident", [P, P], F32)
        blocks = sb("blocks", [P, LAYERS, P], F32)
        film = [sb(f"film{i}", [P, B, 4, C], F32) for i in range(LAYERS)]
        film_now = sb("film_now", [P, 4, C], F32)
        emb = sb("emb", [P, KE, B], F32)
        emb_half = sb("emb_half", [P, KE, B], F32)
        emb_tanh = sb("emb_tanh", [P, KE, B], F32)
        film_f = sb("film_f", [P, 2 * C, B], F32)
        film_g = sb("film_g", [P, C, B], F32)
        film_s = sb("film_s", [P, C, B], F32)
        peak = sb("peak", [P, LAYERS, 8], F32)
        peak_all = sb("peak_all", [P, LAYERS, 8], F32)
        scale_up = sb("scale_up", [P, LAYERS, 8], F32)
        scale_down = sb("scale_down", [P, LAYERS, 8], F32)
        down_o = sb("down_o", [P, LAYERS], F32)
        mask_scale = sb("mask_scale", [P, 1], F32)
        warm = sb("warm", [P, 1], F32)
        k_max = sb("k_max", [P, C], F32)
        k_top = sb("k_top", [P, C], F32)
        k_shift = sb("k_shift", [P, C], F32)
        k_sum = sb("k_sum", [P, C], F32)
        k_recip = sb("k_recip", [P, C], F32)
        q_max = sb("q_max", [P, T, max(HEADS)], F32)
        q_sum = sb("q_sum", [P, T, max(HEADS)], F32)
        q_recip = sb("q_recip", [P, T, max(HEADS)], F32)
        minus_half = sb("minus_half", [P, T], F32)
        x_stats = sb("x_stats", [P, T, 6], F32)
        x_mean_var = sb("x_mean_var", [P, T, 2], F32)
        x_var = sb("x_var", [P, T], F32)
        x_rstd = sb("x_rstd", [P, T], F32)
        x_add = sb("x_add", [P, T], F32)
        y_stats = sb("y_stats", [P, T, 6], F32)
        y_mean_var = sb("y_mean_var", [P, T, 2], F32)
        y_var = sb("y_var", [P, T], F32)
        y_rstd = sb("y_rstd", [P, T], F32)
        y_add = sb("y_add", [P, T], F32)
        v_peak = sb("v_peak", [P, 1], F32)
        y_up = sb("y_up", [P, LAYERS], F32)
        spare = sb("spare", [P, 6], F32)
        ring = [ctx.enter_context(nc.psum_tensor(f"ring{i}", [P, 512], F32)) for i in range(RING)]
        att_ps = ctx.enter_context(nc.psum_tensor("att_ps", [P, C, P], F32))
        film_ps = ctx.enter_context(nc.psum_tensor("film_ps", [P, 512], F32))

        def bank(name, i):
            return ring[slot(name, i)][:]

        last_o = [att_ps[:].rearrange("p c n -> p (c n)"), film_ps[:], bank("O", 0), bank("O'", 3)]

        def flat16(buffer):
            return buffer[:].rearrange("p a b -> p (a b)").bitcast(F16)

        def parts(buffer):
            return flat16(buffer)[:, 0:T * D], flat16(buffer)[:, T * D:2 * T * D]

        def tile(buffer, a, b):
            return buffer[:, (4 * a + b) * P:(4 * a + b + 1) * P]

        kt_hi, kt_lo = parts(kt_or_y)
        qt_hi, qt_lo = parts(k_or_qt)
        v_hi, v_lo = (half.rearrange("p (t d) -> p t d", t=T) for half in parts(v_parts))
        k_lo, q_lo = parts(k_or_qt)[0], flat16(tanh)
        v = q = v_or_q

        def xu(b):
            return x[:, bass.ds(b * T, T), :] if not isinstance(b, int) else x[:, b * T:b * T + T, :]

        def xt(b, t):
            return x[:, bass.ds(b * T + t, 1), :].squeeze(1) if not isinstance(b, int) else x[:, b * T + t, :]

        def batch(unit, layer):
            return unit - layer * B

        last_ht_hi, last_ht_lo = xt_hi, xt_lo

        K_, V_, Q_, O_ = range(4)
        HELD = ((0, 1, 2, 3), (4, 0, 1, 2))
        w_stage2 = wemb.rearrange("p a b c -> p (a b c)").rearrange("p (c n) -> p c n", c=C)
        stages = ((w_stage, kt_or_y, v_parts, w_stage), (w_stage, w_stage2, w_stage, w_stage))
        wemb0 = x[:, 4 * T:8 * T, :].rearrange("p (k h) d -> p k (h d)", k=KE)

        x0_loaded = [sem(f"x0_loaded{t}") for t in range(T)]
        x1_loaded, x_loaded = sem("x1_loaded"), sem("x_loaded")
        emb_loaded = sem("emb_loaded")
        cols_loaded, ident_loaded, tables_loaded = sem("cols_loaded"), sem("ident_loaded"), sem("tables_loaded")
        row_bias_loaded = [sem(f"row_bias_loaded{i}") for i in range(LAYERS)]
        w_loaded = [sem(f"w_loaded{i}") for i in range(4)]
        wemb0_loaded = [sem(f"wemb0_loaded{i}") for i in range(2)]
        wemb_loaded = [sem(f"wemb_loaded{i}") for i in range(2)]
        mask_loaded = sem("mask_loaded")
        bias_o1_loaded, bias_q1_loaded = sem("bias_o1_loaded"), sem("bias_q1_loaded")
        out_stored = sem("out_stored")
        done = {name: sem("pe_" + name) for name, _ in STAGES}
        att_summed = sem("att_summed")
        film_summed = sem("film_summed")
        k_masked, film_read, v_biased = sem("k_masked"), sem("film_read"), sem("v_biased")
        q_biased, xn_ready, x_new = sem("q_biased"), sem("xn_ready"), sem("x_new")
        y_ready = sem("y_ready")
        FREES = {"K": k_masked, "YT": film_read, "V": v_biased, "Q": q_biased, "XT": xn_ready, "O": x_new, "Y": y_ready}
        att_ready, film_ps_read = sem("att_ready"), sem("film_ps_read")
        mask_ready, mask_factor_ready, film_now_ready = sem("mask_ready"), sem("mask_factor_ready"), sem("film_now_ready")
        k_normed = sem("k_normed")
        turn_allowed = sem("turn_allowed")
        k_hi_ready, k_lo_ready, q_hi_ready, q_lo_ready = sem("k_hi_ready"), sem("k_lo_ready"), sem("q_hi_ready"), sem("q_lo_ready")
        kt_hi_ready, kt_lo_ready, qt_hi_ready, qt_lo_ready = (
            sem("kt_hi_ready"), sem("kt_lo_ready"), sem("qt_hi_ready"), sem("qt_lo_ready"))
        v_hi_ready, v_lo_ready = sem("v_hi_ready"), sem("v_lo_ready")
        att_hi_ready, att_lo_ready = sem("att_hi_ready"), sem("att_lo_ready")
        k_top_ready, k_shift_ready, k_exp, k_recip_ready = sem("k_top_ready"), sem("k_shift_ready"), sem("k_exp"), sem("k_recip_ready")
        q_max_ready, q_centred, q_exp, q_summed, q_recip_ready = (
            sem("q_max_ready"), sem("q_centred"), sem("q_exp"), sem("q_summed"), sem("q_recip_ready"))
        x_stats_ready, x_mv_ready, x_var_ready, x_rstd_ready, x_affine_ready = (
            sem("x_stats_ready"), sem("x_mv_ready"), sem("x_var_ready"), sem("x_rstd_ready"), sem("x_affine_ready"))
        y_stats_ready, y_mv_ready, y_var_ready, y_rstd_ready, y_affine_ready = (
            sem("y_stats_ready"), sem("y_mv_ready"), sem("y_var_ready"), sem("y_rstd_ready"), sem("y_affine_ready"))
        q_sum_scaled = sem("q_sum_scaled")
        xh_ready, yh_ready = sem("xh_ready"), sem("yh_ready")
        xt_hi_ready, xt_lo_ready = sem("xt_hi_ready"), sem("xt_lo_ready")
        h_ready, ht_hi_ready, ht_lo_ready, x_biased = sem("h_ready"), sem("ht_hi_ready"), sem("ht_lo_ready"), sem("x_biased")
        w_peak, w_peak_all, w_scale_ready, w_scaled, w_hi_ready = (
            sem("w_peak"), sem("w_peak_all"), sem("w_scale_ready"), sem("w_scaled"), sem("w_hi_ready"))
        w_ready = [sem(f"w_ready{i}") for i in range(LAYERS)]
        film_peak, film_peak_all = sem("film_peak"), sem("film_peak_all")
        ln_peak, ln_peak_all, ln_ready = sem("ln_peak"), sem("ln_peak_all"), sem("ln_ready")
        consts_ready, emb_tanh_ready, emb_ready = sem("consts_ready"), sem("emb_tanh_ready"), sem("emb_ready")
        dve_chain = sem("dve_chain")

        block = ctx.enter_context(nc.Block())

        @block.sync
        def _(sp):
            def load_mask(layer, b):
                src = (mask0_d, mask1_d)[layer]
                row = src[b:b + 1, :] if isinstance(b, int) else src[bass.ds(b, 1), :]
                dst = mask_raw[:] if layer == 0 else mask_raw[:].bitcast(I32)
                sp.dma_start(dst, row.broadcast_to([P, S])).then_inc(mask_loaded, 16)

            def load_w(layer, m):
                if (layer, m) == (0, O_):
                    sp.wait_ge(w_ready[0], K_ + 1)
                elif (layer, m) == (1, K_):
                    sp.wait_ge(w_ready[0], O_ + 1)
                elif (layer, m) == (1, Q_):
                    sp.wait_ge(w_ready[1], K_ + 1)
                elif (layer, m) == (1, O_):
                    sp.wait_ge(w_ready[1], Q_ + 1)
                sp.dma_start(stages[layer][m][:], w_d[layer][m].rearrange("(c p) n -> p c n", p=P)).then_inc(w_loaded[m], 16)

            def load_row(dst, src, loaded):
                sp.dma_start(dst, src.rearrange("(a d) -> a d", a=1).broadcast_to([P, D])).then_inc(loaded, 16)

            def load_wemb0(begin, end):
                sp.dma_start(wemb0[:, :, begin:end], wemb_d[0].rearrange("(k p) n -> p k n", p=P)[:, :, begin:end]
                             ).then_inc(wemb0_loaded[begin > 0], 16)

            def load_wemb1(js):
                for j in js:
                    if j == 0:
                        sp.wait_ge(w_ready[1], V_ + 1)
                    if j >= 2:
                        sp.wait_ge(film_summed, 2 * C + j - 1)
                    sp.dma_start(wemb[:, j % 2], wemb_d[1].rearrange("(k p) n -> p k n", p=P)[:, :, j * P:j * P + P]
                                 ).then_inc(wemb_loaded[j % 2], 16)

            def turn(out, source, ready, value, turned):
                sp.wait_ge(ready, value)
                sp.sem_inc(turn_allowed, 1)
                sp.dma_start_transpose(out.rearrange("p (n m) -> p n m", m=P), source).then_inc(turned, 16)

            def step(u, back, following, film=False):
                if following is not None:
                    sp.wait_ge(k_normed, 4 * (u + 1))
                    load_mask(following, batch(u + 1, following))
                if back is not None:
                    sp.wait_ge(done["YT"], 4 * u)
                else:
                    sp.wait_ge(w_ready[0], V_ + 1)
                if film:
                    load_wemb1((2, 3))
                    load_w(1, O_)
                turn(kt_hi, kq_hi[:], k_hi_ready, 4 * (u + 1), kt_hi_ready)
                if film:
                    load_wemb1((4, 5))
                turn(kt_lo, k_lo, k_lo_ready, 4 * (u + 1), kt_lo_ready)
                if film:
                    load_wemb1((6, 7))
                if isinstance(u, int) and u == B - 1:
                    sp.wait_ge(q_biased, 4 * B)
                    load_row(bias_q[:], bias_d[1][1], bias_q1_loaded)
                sp.wait_ge(kt_hi_ready, 16 * (u + 1))
                sp.wait_ge(kt_lo_ready, 16 * (u + 1))
                turn(qt_hi, kq_hi[:], q_hi_ready, 4 * (u + 1), qt_hi_ready)
                turn(qt_lo, q_lo, q_lo_ready, 4 * (u + 1), qt_lo_ready)
                if back == 1:
                    sp.wait_ge(x_new, 4 * u)
                    store(batch(u - 1, 1))

            def store(b):
                dst = out_d[b] if isinstance(b, int) else out_d[bass.ds(b, 1)].squeeze(0)
                sp.dma_start(dst.rearrange("(t p) d -> p t d", p=P), xu(b)).then_inc(out_stored, 16)

            def load_x(b, loaded):
                sp.dma_start(xu(b), x_d[b].rearrange("(t p) d -> p t d", p=P)).then_inc(loaded, 16)

            for t in range(T):
                sp.dma_start(xt(0, t), x_d[0, t * P:t * P + P, :]).then_inc(x0_loaded[t], 16)
                if t == 1:
                    sp.dma_start(cols[:], cols_d).then_inc(cols_loaded, 16)
            sp.dma_start(ident[:], ident_d).then_inc(ident_loaded, 16)
            sp.dma_start(emb[:], emb_d).then_inc(emb_loaded, 16)
            load_w(0, K_)
            load_wemb0(0, 2 * P)
            sp.dma_start(blocks[:], blocks_d).then_inc(tables_loaded, 16)
            load_w(0, V_)
            load_mask(0, 0)
            load_w(0, Q_)
            for dst, src in zip((bias_v[0], bias_q, bias_o), bias_d[0]):
                load_row(dst[:], src, row_bias_loaded[0])
            load_x(1, x1_loaded)
            load_wemb0(2 * P, 2 * D)
            load_w(0, O_)
            load_row(bias_v[1][:], bias_d[1][0], row_bias_loaded[1])
            for b in range(2, 4):
                load_x(b, x_loaded)
            step(0, None, 0)
            load_w(1, V_)
            sp.wait_ge(film_summed, 2 * C)
            for b in range(4, B):
                load_x(b, x_loaded)
            load_w(1, K_)
            with sp.Fori(1, B - 1) as u:
                step(u, 0, 0)
            sp.wait_ge(x_biased, B)
            load_row(bias_o[:], bias_d[1][2], bias_o1_loaded)
            step(B - 1, 0, 1)
            load_w(1, Q_)
            load_wemb1(range(2))
            step(B, 0, 1, film=True)
            with sp.Fori(B + 1, UNITS - 1) as u:
                step(u, 1, 1)
            step(UNITS - 1, 1, None)
            for t in range(T):
                sp.wait_ge(x_new, 4 * (UNITS - 1) + t + 1)
                sp.dma_start(out_d[B - 1, t * P:t * P + P, :], xt(B - 1, t)).then_inc(out_stored, 16)
            sp.wait_ge(out_stored, 16 * (B - 1 + T))

        @block.tensor
        def _(pe):
            def take_bank(name, i, u):
                before = previous_user(name, i, u)
                if before is not None:
                    stage, n, unit = before
                    pe.wait_ge(FREES[stage], 4 * unit + n + 1)
                return bank(name, i)

            def product(out, pairs):
                for n, (lhs, rhs) in enumerate(pairs):
                    last = nc.tensor.matmul(out, lhs, rhs, start=(n == 0), stop=(n == len(pairs) - 1))
                return last

            def split_pairs(lhs_hi, lhs_lo, rhs_hi, rhs_lo):
                return [p for c in range(C) for p in ((lhs_hi(c), rhs_hi(c)), (lhs_hi(c), rhs_lo(c)), (lhs_lo(c), rhs_hi(c)))]

            def nothing(i):
                pass

            def project_features(name, u, m, layer, between=nothing):
                hi, lo = w_hi[HELD[layer][m]], w_lo[HELD[layer][m]]
                for i in range(C):
                    f = slice(i * P, i * P + P)
                    out = take_bank(name, i, u)
                    product(out, split_pairs(lambda c: hi[:, c, f], lambda c: lo[:, c, f],
                                             lambda c: xt_hi[:, c, :], lambda c: xt_lo[:, c, :])).then_inc(done[name], 1)
                    between(i)

            def project_tokens(name, u, m, layer, a_hi, a_lo, tiles=range(T), between=nothing):
                hi, lo = w_hi[HELD[layer][m]], w_lo[HELD[layer][m]]
                for i in tiles:
                    s = slice(i * P, i * P + P)
                    out = take_bank(name, i, u)
                    product(out, split_pairs(lambda c: a_hi[:, c, s], lambda c: a_lo[:, c, s],
                                             lambda c: hi[:, c, :], lambda c: lo[:, c, :])).then_inc(done[name.rstrip("'")], 1)
                    between(i)

            def turn(name, i, u, source):
                out = take_bank(name, i, u)
                for j in range(4):
                    last = nc.tensor.transpose(out[:, j * P:j * P + P], source(i, j), ident[:])
                last.then_inc(done[name], 1)

            def turn_x(u):
                for i in range(C):
                    if i == 0:
                        pe.wait_ge(xh_ready, 4 * (u + 2))
                    turn("XT", i, u, lambda c, t: xh_or_h[:, t, c * P:c * P + P])

            def sum_film(layer, js):
                if 0 in js:
                    if layer == 0:
                        pe.wait_ge(emb_ready, 1)
                    else:
                        pe.wait_ge(film_ps_read, 1)
                for j in js:
                    if layer == 0:
                        pe.wait_ge(wemb0_loaded[j > 1], 16)
                        w = wemb0[:, :, j * P:j * P + P]
                    else:
                        pe.wait_ge(wemb_loaded[j % 2], 16 * (j // 2 + 1))
                        w = wemb[:, j % 2]
                    product(film_ps[:, j * B:j * B + B], [(w[:, k, :], emb[:, k, :]) for k in range(KE)]
                            ).then_inc(film_summed, 1)

            def attend(u):
                pe.wait_ge(qt_hi_ready, 16 * (u + 1))
                pe.wait_ge(qt_lo_ready, 16 * (u + 1))
                pe.wait_ge(att_lo_ready, u + 1)
                for t in range(T):
                    out = take_bank("Y", t, u)
                    for c in range(C):
                        hi, lo = tile(qt_hi, t, c), tile(qt_lo, t, c)
                        last = product(out[:, c * P:c * P + P], [(hi, att_hi[:, c, :]), (hi, att_lo[:, c, :]), (lo, att_hi[:, c, :])])
                    last.then_inc(done["Y"], 1)

            def step(u, front, back, following, first=False):
                def film_after(n):
                    return (lambda i: sum_film(front, [n + i] if n + i < (4, 2 * C)[front] else [])) if first else nothing

                pe.wait_ge(xt_lo_ready, 4 * (u + 1))
                if first:
                    pe.wait_ge(w_ready[front], K_ + 1)
                project_features("K", u, K_, front)
                if back is not None:
                    pe.wait_ge(yh_ready, 4 * u)
                    for i in range(C):
                        turn("YT", i, u, lambda c, t: kt_or_y[:, t, c * P:c * P + P])
                if first:
                    pe.wait_ge(w_ready[front], V_ + 1)
                project_tokens("V", u, V_, front, xt_hi, xt_lo, between=film_after((2, 0)[front]))
                if first:
                    pe.wait_ge(w_ready[front], Q_ + 1)
                project_tokens("Q", u, Q_, front, xt_hi, xt_lo, between=film_after((6, 4)[front]))
                pe.wait_ge(kt_hi_ready, 16 * (u + 1))
                pe.wait_ge(kt_lo_ready, 16 * (u + 1))
                pe.wait_ge(v_lo_ready, 4 * (u + 1))
                if not isinstance(u, int) or u:
                    pe.wait_ge(att_ready, u)
                for c in range(C):
                    f = slice(c * P, c * P + P)
                    k_parts = (lambda t: tile(kt_hi, c, t), lambda t: tile(kt_lo, c, t))
                    v_parts_t = (lambda t: v_hi[:, t, f], lambda t: v_lo[:, t, f])
                    left, right = (k_parts, v_parts_t) if front == 0 else (v_parts_t, k_parts)
                    last = product(att_ps[:, c, :], split_pairs(*left, *right))
                last.then_inc(att_summed, 1)
                if following is not None:
                    turn_x(u)
                if first and front == 0:
                    sum_film(0, range(4, 2 * C))
                if back is not None:
                    pe.wait_ge(ht_lo_ready, 4 * u)
                    pe.wait_ge(w_ready[back], O_ + 1)
                    project_tokens("O", u, O_, back, ht_hi, ht_lo, range(T if following is not None else T - 1))
                attend(u)

            def last_step(u, layer):
                banks = [take_bank("YT", i, u) for i in range(C)]
                for t in range(T):
                    pe.wait_ge(yh_ready, 4 * (u - 1) + t + 1)
                    for i in range(C):
                        turned = nc.tensor.transpose(banks[i][:, t * P:t * P + P], kt_or_y[:, t, i * P:i * P + P], ident[:])
                        if t == T - 1:
                            turned.then_inc(done["YT"], 1)
                project_tokens("O'", u, O_, layer, ht_hi, ht_lo, (T - 1,))
                hi, lo = w_hi[HELD[layer][O_]], w_lo[HELD[layer][O_]]
                pe.wait_ge(att_ready, UNITS)
                pe.wait_ge(film_ps_read, LAYERS)
                pe.wait_ge(x_new, 4 * (UNITS - 2) + 3)
                for c in range(C):
                    pe.wait_ge(ht_hi_ready, 4 * (u - 1) + c + 1)
                    for i in range(T):
                        s = slice(i * P, i * P + P)
                        if c == 0 and i == T - 1:
                            pe.wait_ge(x_new, 4 * (UNITS - 1))
                        nc.tensor.matmul(last_o[i], last_ht_hi[:, c, s], hi[:, c, :], start=(c == 0), stop=False)
                        nc.tensor.matmul(last_o[i], last_ht_hi[:, c, s], lo[:, c, :], start=False, stop=False)
                    pe.wait_ge(ht_lo_ready, 4 * (u - 1) + c + 1)
                    for i in range(T):
                        s = slice(i * P, i * P + P)
                        last = nc.tensor.matmul(last_o[i], last_ht_lo[:, c, s], hi[:, c, :], start=False, stop=(c == C - 1))
                        if c == C - 1:
                            last.then_inc(done["O"], 1)

            pe.wait_ge(ident_loaded, 16)
            turn_x(-1)
            sum_film(0, (0, 1))
            step(0, 0, None, 0, first=True)
            with pe.Fori(1, B - 1) as u:
                step(u, 0, 0, 0)
            step(B - 1, 0, 0, 1)
            step(B, 1, 0, 1, first=True)
            with pe.Fori(B + 1, UNITS - 1) as u:
                step(u, 1, 1, 1)
            step(UNITS - 1, 1, 1, None)
            last_step(UNITS, 1)

        @block.vector
        def _(dve):
            links = [0]

            def link(ins):
                links[0] += 1
                ins.then_inc(dve_chain, 1)
                dve.wait_ge(dve_chain, links[0])

            def wait_here(semaphore, value, word):
                dve.wait_ge(semaphore, value)
                nc.vector.memset(spare[:, word:word + 1], 0.0)

            def power(layer, n):
                at = (slice(None), layer, slice(n, n + 1))
                link(nc.vector.tensor_scalar(scale_down[at].bitcast(I32), peak_all[at].bitcast(I32), EXP_BITS, None, ALU.bitwise_and))
                link(nc.vector.tensor_scalar(scale_up[at].bitcast(I32), scale_down[at].bitcast(I32), EXP_BITS, None, ALU.bitwise_xor))

            def find_peak(layer, m):
                dve.wait_ge(w_loaded[m], 16 * (layer + 1))
                at = peak[:, layer, m:m + 1]
                link(nc.vector.tensor_reduce(at, stages[layer][m][:].rearrange("p c n -> p (c n)"), AX_X, ALU.max,
                                             apply_absolute_value=True))
                nc.vector.tensor_scalar(at, at, TINY, None, ALU.max).then_inc(w_peak, 1)

            def find_scale(layer, m):
                dve.wait_ge(w_peak_all, 4 * layer + m + 1)
                power(layer, m)
                up, down = scale_up[:, layer, m:m + 1], scale_down[:, layer, m:m + 1]
                nc.vector.tensor_scalar(up, up, UP, None, ALU.mult).then_inc(w_scale_ready, 1)
                if m == O_:
                    link(nc.vector.tensor_scalar(down, down, 0.5 / UP, None, ALU.mult))
                else:
                    link(nc.vector.tensor_scalar(down, down, 0.5 / UP, scale_down[:, layer, LN:LN + 1], ALU.mult, ALU.mult))
                if layer == 0 and m == K_:
                    dve.wait_ge(w_scale_ready, 1)
                    link(nc.vector.tensor_scalar(mask_scale[:], up, scale_up[:, layer, LN:LN + 1], MASK_ADD, ALU.mult, ALU.mult))

            def v_scales(layer):
                bound = peak_all[:, layer, V_BOUND:V_BOUND + 1]
                link(nc.vector.tensor_reduce(bound, bias_v[layer][:], AX_X, ALU.max, apply_absolute_value=True))
                link(nc.vector.tensor_scalar(v_peak[:], peak_all[:, layer, V_:V_ + 1], float(D), peak_all[:, layer, LN:LN + 1],
                                             ALU.mult, ALU.mult))
                link(nc.vector.tensor_tensor(bound, bound, v_peak[:], ALU.add))
                power(layer, V_BOUND)
                up, down = scale_up[:, layer, V_BOUND:V_BOUND + 1], scale_down[:, layer, V_:V_ + 1]
                link(nc.vector.tensor_scalar(up, up, UP, None, ALU.mult))
                link(nc.vector.tensor_scalar(down, down, up, None, ALU.mult))
                link(nc.vector.tensor_scalar(y_up[:, layer:layer + 1], up, ONE, None, ALU.mult))
                link(nc.vector.tensor_scalar(bias_v[layer][:], bias_v[layer][:], up, None, ALU.mult))

            def split_low(m):
                for c in range(C):
                    dve.wait_ge(w_hi_ready, 4 * m + c + 1)
                    last = nc.vector.scalar_tensor_tensor(out=w_lo[m][:, c, :], in0=stages[0][m][:, c, :],
                                                          scalar=scale_up[:, 0, m:m + 1], in1=w_hi[m][:, c, :],
                                                          op0=ALU.mult, op1=ALU.subtract)
                last.then_inc(w_ready[0], 1)

            def ln_peaks(layer):
                for n, at in ((4, LN_W), (5, LN_B)):
                    link(nc.vector.tensor_reduce(peak[:, layer, n:n + 1], cols[:, layer, at:at + C], AX_X, ALU.max,
                                                 apply_absolute_value=True))
                at = peak[:, layer, LN:LN + 1]
                link(nc.vector.scalar_tensor_tensor(out=at, in0=peak[:, layer, 4:5], scalar=NORM_MAX,
                                                    in1=peak[:, layer, 5:6], op0=ALU.mult, op1=ALU.add))
                nc.vector.tensor_scalar(at, at, TINY, None, ALU.max).then_inc(ln_peak, 1)

            def ln_scales(layer):
                dve.wait_ge(ln_peak_all, layer + 1)
                power(layer, LN)
                up, down = scale_up[:, layer, LN:LN + 1], scale_down[:, layer, LN:LN + 1]
                link(nc.vector.tensor_scalar(up, up, UP, None, ALU.mult))
                link(nc.vector.tensor_scalar(down, down, 0.5 / UP, None, ALU.mult))
                nc.vector.tensor_scalar(ln_now[:, layer, 0, :], cols[:, layer, LN_W:LN_W + C], up, None, ALU.mult).then_inc(ln_ready, 1)
                nc.vector.tensor_scalar(ln_now[:, layer, 1, :], cols[:, layer, LN_B:LN_B + C], up, None, ALU.mult).then_inc(ln_ready, 1)

            def prepare_film(layer):
                wide = lambda at: cols[:, layer, at:at + C].unsqueeze(2).broadcast_to([P, C, B])
                dve.wait_ge(film_summed, 2 * C * (layer + 1))
                ins = nc.vector.tensor_tensor(film_f[:], film_ps[:, 0:2 * C * B].rearrange("p (j b) -> p j b", b=B),
                                              cols[:, layer, B_EMB:B_EMB + 2 * C].unsqueeze(2).broadcast_to([P, 2 * C, B]), ALU.add)
                ins.then_inc(film_ps_read, 1)
                dve.wait_ge(film_ps_read, layer + 1)
                link(nc.vector.tensor_scalar(film_f[:, 0:C, :], film_f[:, 0:C, :], 1.0, None, ALU.add))
                link(nc.vector.tensor_tensor(film_g[:], film_f[:, 0:C, :], wide(LN2_W), ALU.mult))
                link(nc.vector.tensor_tensor(film_s[:], film_f[:, 0:C, :], wide(LN2_B), ALU.mult))
                link(nc.vector.tensor_tensor(film_s[:], film_s[:], film_f[:, C:2 * C, :], ALU.add))
                link(nc.vector.tensor_reduce(peak[:, layer, 4:5], film_g[:].rearrange("p c b -> p (c b)"), AX_X, ALU.max,
                                             apply_absolute_value=True))
                link(nc.vector.tensor_reduce(peak[:, layer, 5:6], film_s[:].rearrange("p c b -> p (c b)"), AX_X, ALU.max,
                                             apply_absolute_value=True))
                link(nc.vector.scalar_tensor_tensor(out=peak[:, layer, 6:7], in0=peak[:, layer, 4:5], scalar=NORM_MAX,
                                                    in1=peak[:, layer, 5:6], op0=ALU.mult, op1=ALU.add))
                nc.vector.tensor_scalar(peak[:, layer, 6:7], peak[:, layer, 6:7], TINY, None, ALU.max).then_inc(film_peak, 1)
                dve.wait_ge(film_peak_all, layer + 1)
                power(layer, 6)
                link(nc.vector.tensor_scalar(scale_up[:, layer, 6:7], scale_up[:, layer, 6:7], UP, None, ALU.mult))
                link(nc.vector.tensor_scalar(scale_down[:, layer, 6:7], scale_down[:, layer, 6:7], 0.5 / UP, None, ALU.mult))
                table = lambda kind: film[layer][:, :, kind, :].rearrange("p b c -> p c b")
                up = scale_up[:, layer, 6:7]
                link(nc.vector.tensor_scalar(table(0), film_g[:], 0.5, None, ALU.mult))
                link(nc.vector.tensor_scalar(table(1), film_s[:], 0.5, None, ALU.mult))
                link(nc.vector.tensor_scalar(table(2), film_g[:], 0.5, up, ALU.mult, ALU.mult))
                link(nc.vector.tensor_scalar(table(3), film_s[:], 0.5, up, ALU.mult, ALU.mult))

            def output_scale(layer):
                link(nc.vector.tensor_tensor(down_o[:, layer:layer + 1], scale_down[:, layer, O_:O_ + 1],
                                             scale_down[:, layer, 6:7], ALU.mult))

            def x_statistics(unit, layer):
                b = batch(unit, layer)
                if layer == 1:
                    dve.wait_ge(x_new, 4 * (b + 1))
                for t in range(T):
                    if isinstance(unit, int) and unit == 0:
                        dve.wait_ge(x0_loaded[t], 16)
                    nc.vector.bn_stats(x_stats[:, t, :], xt(b, t)).then_inc(x_stats_ready, 1)
                wait_here(x_stats_ready, 4 * (unit + 1), 4)
                for t in range(T):
                    nc.vector.bn_aggr(x_mean_var[:, t, :], x_stats[:, t, :]).then_inc(x_mv_ready, 1)
                dve.wait_ge(x_mv_ready, 4 * (unit + 1))
                nc.vector.tensor_scalar(x_var[:], x_mean_var[:, :, 1], EPS, None, ALU.add).then_inc(x_var_ready, 1)

            def x_affine(unit):
                dve.wait_ge(x_rstd_ready, unit + 1)
                nc.vector.scalar_tensor_tensor(out=x_add[:], in0=x_mean_var[:, :, 0], scalar=-1.0, in1=x_rstd[:],
                                               op0=ALU.mult, op1=ALU.mult).then_inc(x_affine_ready, 1)

            def step(u, front, back, following, prep=None):
                u_is_first = isinstance(u, int) and u == 0

                def residual(tiles, unit, banks=[bank("O", t) for t in range(T)]):
                    dve.wait_ge(x_biased, unit + 1)
                    b = batch(unit, back)
                    for t in tiles:
                        dve.wait_ge(done["O"], 4 * unit + t + 1)
                        nc.vector.scalar_tensor_tensor(out=xt(b, t), in0=banks[t], scalar=down_o[:, back:back + 1],
                                                       in1=xt(b, t), op0=ALU.mult, op1=ALU.add).then_inc(x_new, 1)

                if back is not None:
                    b = batch(u - 1, back)
                    src = film[back][:, b] if isinstance(b, int) else film[back][:, bass.ds(b, 1)].squeeze(1)
                    nc.vector.tensor_copy(film_now[:], src).then_inc(film_now_ready, 1)
                if prep == 1:
                    find_peak(1, K_)
                if front is not None:
                    heads = HEADS[front]
                    dve.wait_ge(mask_loaded, 16 * (u + 1))
                    if front == 0:
                        nc.vector.tensor_scalar(mask_add[:], mask_raw[:], 1.0, mask_scale[:], ALU.subtract, ALU.mult
                                                ).then_inc(mask_ready, 1)
                        nc.vector.tensor_scalar(mask_raw[:], mask_raw[:], ONE, None, ALU.mult).then_inc(mask_factor_ready, 1)
                    else:
                        mask_int = mask_raw[:].bitcast(I32)
                        nc.vector.tensor_scalar(mask_add[:], mask_int, 1.0, MASKED_OUT, ALU.is_equal, ALU.mult
                                                ).then_inc(mask_ready, 1)
                        nc.vector.tensor_scalar(mask_raw[:], mask_int, 1.0, ONE, ALU.not_equal, ALU.mult
                                                ).then_inc(mask_factor_ready, 1)
                    if prep:
                        find_scale(1, K_ if prep == 1 else Q_)
                    dve.wait_ge(mask_ready, u + 1)
                    for i in range(C):
                        wait_here(done["K"], 4 * u + i + 1, i)
                        nc.vector.tensor_tensor_reduce(k_or_qt[:, i, :], bank("K", i), mask_add[:],
                                                       scale_down[:, front, K_:K_ + 1], -3.4e38, ALU.add, ALU.max,
                                                       k_max[:, i:i + 1]).then_inc(k_masked, 1)
                    bias_k = cols[:, front, B_K:B_K + C]
                    dve.wait_ge(k_masked, 4 * (u + 1))
                    nc.vector.tensor_tensor(k_top[:], k_max[:], bias_k, ALU.add).then_inc(k_top_ready, 1)
                    dve.wait_ge(k_top_ready, u + 1)
                    nc.vector.tensor_tensor(k_shift[:], bias_k, k_top[:], ALU.subtract).then_inc(k_shift_ready, 1)
                if following is not None:
                    x_statistics(u + 1, following)
                if u_is_first:
                    ln_peaks(1)
                if front is not None:
                    dve.wait_ge(k_exp, 4 * (u + 1))
                    nc.vector.reciprocal(k_recip[:], k_sum[:]).then_inc(k_recip_ready, 1)
                    dve.wait_ge(k_recip_ready, u + 1)
                    dve.wait_ge(mask_factor_ready, u + 1)
                    for i in range(C):
                        if front == 0:
                            ins = nc.vector.tensor_tensor(k_or_qt[:, i, :], k_or_qt[:, i, :], mask_raw[:], ALU.mult)
                        else:
                            ins = nc.vector.scalar_tensor_tensor(out=k_or_qt[:, i, :], in0=k_or_qt[:, i, :],
                                                                 scalar=k_recip[:, i:i + 1], in1=mask_raw[:],
                                                                 op0=ALU.mult, op1=ALU.mult)
                        ins.then_inc(k_normed, 1)
                def split_k():
                    for i in range(C):
                        dve.wait_ge(k_hi_ready, 4 * u + i + 1)
                        if i:
                            dve.wait_ge(k_lo_ready, 4 * u + i)
                        nc.vector.tensor_tensor(k_lo[:, i * S:i * S + S], k_or_qt[:, i, :], kq_hi[:, i * S:i * S + S], ALU.subtract
                                                ).then_inc(k_lo_ready, 1)

                if back is None:
                    split_k()
                if back is not None:
                    for c in range(C):
                        if c == 2 and front is not None:
                            split_k()
                        if front is None:
                            dve.wait_ge(film_read, 4 * (u - 1) + c + 1)
                            link(nc.vector.tensor_scalar(xh_or_h[:, c, :], bank("YT", c), film_now[:, 2, c:c + 1],
                                                         film_now[:, 3, c:c + 1], ALU.mult, ALU.add))
                            if c == 1:
                                residual((T - 1,), u - 2, {T - 1: bank("O'", T - 1)})
                        else:
                            dve.wait_ge(film_read, 4 * (u - 1) + c + 1)
                        nc.vector.scalar_tensor_tensor(out=xh_or_h[:, c, :], in0=tanh[:, c % 2, :], scalar=1.0,
                                                       in1=xh_or_h[:, c, :], op0=ALU.add, op1=ALU.mult).then_inc(h_ready, 1)
                    if front is None:
                        residual(range(T), u - 1, last_o)
                if u_is_first:
                    split_low(Q_)
                    ln_scales(1)
                if front is not None:
                    for t in range(T):
                        dve.wait_ge(done["V"], 4 * u + t + 1)
                        nc.vector.scalar_tensor_tensor(out=v[:, t, :], in0=bank("V", t), scalar=scale_down[:, front, V_:V_ + 1],
                                                       in1=bias_v[front][:], op0=ALU.mult, op1=ALU.add).then_inc(v_biased, 1)
                if u_is_first:
                    find_peak(0, O_)
                if following is not None:
                    x_affine(u + 1)
                if u_is_first:
                    find_scale(0, O_)
                if front is not None:
                    by_head = lambda a: a.rearrange("p (h e) -> p h e", h=heads)
                    wide = lambda a: a.unsqueeze(2).broadcast_to([P, heads, D // heads])

                    def low_q(t):
                        dve.wait_ge(q_hi_ready, 4 * u + t + 1)
                        nc.vector.scalar_tensor_tensor(out=q_lo[:, t * D:t * D + D], in0=q[:, t, :], scalar=ONE,
                                                       in1=kq_hi[:, t * D:t * D + D], op0=ALU.mult, op1=ALU.subtract
                                                       ).then_inc(q_lo_ready, 1)

                    if prep == 2:
                        dve.wait_ge(bias_q1_loaded, 16)
                    for t in range(T):
                        dve.wait_ge(v_lo_ready, 4 * u + t + 1)
                        dve.wait_ge(done["Q"], 4 * u + t + 1)
                        nc.vector.scalar_tensor_tensor(out=q[:, t, :], in0=bank("Q", t), scalar=scale_down[:, front, Q_:Q_ + 1],
                                                       in1=bias_q[:], op0=ALU.mult, op1=ALU.add).then_inc(q_biased, 1)
                        dve.wait_ge(q_biased, 4 * u + t + 1)
                        nc.vector.tensor_reduce(q_max[:, t, 0:heads], by_head(q[:, t, :]), AX_X, ALU.max).then_inc(q_max_ready, 1)
                        dve.wait_ge(q_max_ready, 4 * u + t + 1)
                        nc.vector.tensor_tensor(by_head(q[:, t, :]), by_head(q[:, t, :]), wide(q_max[:, t, 0:heads]),
                                                ALU.subtract).then_inc(q_centred, 1)
                        if t:
                            low_q(t - 1)
                if front is not None:
                    dve.wait_ge(att_summed, u + 1)
                    if front == 0:
                        for c in range(C):
                            last = nc.vector.scalar_tensor_tensor(out=att[:, c, :], in0=att_ps[:, c, :],
                                                                  scalar=k_recip[:, c:c + 1], in1=blocks[:, 0, :],
                                                                  op0=ALU.mult, op1=ALU.mult)
                    else:
                        last = nc.vector.tensor_tensor(att[:], att_ps[:], blocks[:, 1:2, :].broadcast_to([P, C, P]), ALU.mult)
                    last.then_inc(att_ready, 1)
                    low_q(T - 1)
                    for t in range(T):
                        nc.vector.tensor_reduce(q_sum[:, t, 0:heads], by_head(q[:, t, :]), AX_X, ALU.add).then_inc(q_summed, 1)
                    dve.wait_ge(q_summed, 4 * (u + 1))
                    nc.vector.tensor_scalar(q_sum[:, :, 0:heads], q_sum[:, :, 0:heads], y_up[:, front:front + 1], None, ALU.mult
                                            ).then_inc(q_sum_scaled, 1)
                    dve.wait_ge(q_sum_scaled, u + 1)
                    nc.vector.reciprocal(q_recip[:, :, 0:heads], q_sum[:, :, 0:heads]).then_inc(q_recip_ready, 1)
                if prep == 1:
                    find_peak(1, V_)
                if prep == 2:
                    prepare_film(1)

                if back is not None and following is not None:
                    residual(range(2), u - 1)
                if prep == 2:
                    find_peak(1, O_)
                if prep == 1:
                    find_scale(1, V_)
                if back is not None and following is not None:
                    residual((2,), u - 1)
                if prep == 2:
                    find_scale(1, O_)
                    output_scale(1)
                if back is not None and following is not None:
                    residual((3,), u - 1)
                if front is not None and following is None:
                    residual(range(T - 1), u - 1)
                if front is not None:
                    dve.wait_ge(q_recip_ready, u + 1)
                    for t in range(T + 1):
                        if t < T:
                            dve.wait_ge(done["Y"], 4 * u + t + 1)
                            nc.vector.tensor_tensor(by_head(kt_or_y[:, t, :]), by_head(bank("Y", t)),
                                                    wide(q_recip[:, t, 0:heads]), ALU.mult).then_inc(y_ready, 1)
                        if t:
                            dve.wait_ge(y_ready, 4 * u + t)
                            nc.vector.bn_stats(y_stats[:, t - 1, :], kt_or_y[:, t - 1, :]).then_inc(y_stats_ready, 1)
                    wait_here(y_stats_ready, 4 * (u + 1), 5)
                    for t in range(T):
                        nc.vector.bn_aggr(y_mean_var[:, t, :], y_stats[:, t, :]).then_inc(y_mv_ready, 1)
                    dve.wait_ge(y_mv_ready, 4 * (u + 1))
                    nc.vector.tensor_scalar(y_var[:], y_mean_var[:, :, 1], EPS, None, ALU.add).then_inc(y_var_ready, 1)
                    dve.wait_ge(y_rstd_ready, u + 1)
                    nc.vector.scalar_tensor_tensor(out=y_add[:], in0=y_mean_var[:, :, 0], scalar=-1.0, in1=y_rstd[:],
                                                   op0=ALU.mult, op1=ALU.mult).then_inc(y_affine_ready, 1)
                if u_is_first:
                    prepare_film(0)
                    output_scale(0)
                    split_low(O_)
                if prep == 1:
                    v_scales(1)
                    find_peak(1, Q_)

            nc.vector.memset(minus_half[:], -0.5).then_inc(consts_ready, 1)
            x_statistics(0, 0)
            dve.wait_ge(cols_loaded, 16)
            ln_peaks(0)
            x_affine(0)
            ln_scales(0)
            dve.wait_ge(emb_loaded, 16)
            link(nc.vector.tensor_scalar(emb_half[:], emb[:], 0.5, None, ALU.mult))
            dve.wait_ge(emb_tanh_ready, 1)
            nc.vector.scalar_tensor_tensor(out=emb[:], in0=emb_tanh[:], scalar=1.0, in1=emb_half[:], op0=ALU.add, op1=ALU.mult
                                           ).then_inc(emb_ready, 1)
            find_peak(0, K_)
            dve.wait_ge(tables_loaded, 16)
            find_scale(0, K_)
            split_low(K_)
            find_peak(0, V_)
            for c in range(C):
                dve.wait_ge(xt_hi_ready, c + 1)
                nc.vector.tensor_tensor(xt_lo[:, c, :], xh_or_h[:, c, :], xt_hi[:, c, :], ALU.subtract).then_inc(xt_lo_ready, 1)
            find_scale(0, V_)
            find_peak(0, Q_)
            split_low(V_)
            find_scale(0, Q_)
            dve.wait_ge(row_bias_loaded[0], 48)
            v_scales(0)
            dve.wait_ge(x1_loaded, 16)
            step(0, 0, None, 0)
            dve.wait_ge(row_bias_loaded[1], 16)
            dve.wait_ge(x_loaded, 16 * (B - 2))
            with dve.Fori(1, B - 1) as u:
                step(u, 0, 0, 0)
            step(B - 1, 0, 0, 1, prep=1)
            step(B, 1, 0, 1, prep=2)
            with dve.Fori(B + 1, UNITS - 1) as u:
                step(u, 1, 1, 1)
            step(UNITS - 1, 1, 1, None)
            step(UNITS, None, 1, None)

        @block.scalar
        def _(act):
            def split_high(layer, m):
                act.wait_ge(w_scale_ready, 4 * layer + m + 1)
                if layer == 1 and m != K_:
                    act.wait_ge(done[("K", "V", "Q")[HELD[1][m]]], 4 * B)
                hi, w, up = w_hi[HELD[layer][m]], stages[layer][m], scale_up[:, layer, m:m + 1]
                if layer == 0:
                    for c in range(C):
                        nc.scalar.activation(hi[:, c, :], w[:, c, :], ACT.Copy, scale=up).then_inc(w_hi_ready, 1)
                else:
                    for c in range(C):
                        nc.scalar.activation(w[:, c, :], w[:, c, :], ACT.Copy, scale=up).then_inc(w_scaled, 1)
                    for c in range(C):
                        act.wait_ge(w_scaled, 4 * m + c + 1)
                        nc.scalar.copy(hi[:, c, :], w[:, c, :]).then_inc(w_hi_ready, 1)

            def normalise_x(unit, layer, after_h):
                b = batch(unit, layer)
                act.wait_ge(x_affine_ready, unit + 1)
                if after_h is not None:
                    act.wait_ge(ht_lo_ready, 4 * after_h)
                elif unit:
                    act.wait_ge(xt_lo_ready, 4 * unit)
                for t in range(T):
                    nc.scalar.activation(xh_or_h[:, t, :], xt(b, t), ACT.Identity, bias=x_add[:, t:t + 1],
                                         scale=x_rstd[:, t:t + 1]).then_inc(xh_ready, 1)

            def turned_x(unit, layer):
                act.wait_ge(done["XT"], 4 * (unit + 1))
                for c in range(C):
                    nc.scalar.activation(xh_or_h[:, c, :], bank("XT", c), ACT.Identity, bias=ln_now[:, layer, 1, c:c + 1],
                                         scale=ln_now[:, layer, 0, c:c + 1]).then_inc(xn_ready, 1)
                for c in range(C):
                    act.wait_ge(xn_ready, 4 * unit + c + 1)
                    nc.scalar.copy(xt_hi[:, c, :], xh_or_h[:, c, :]).then_inc(xt_hi_ready, 1)

            def step(u, front, back, following, prep=None):
                def high(c):
                    act.wait_ge(h_ready, 4 * (u - 1) + c + 1)
                    nc.scalar.copy((ht_hi if front is not None else last_ht_hi)[:, c, :], xh_or_h[:, c, :]).then_inc(ht_hi_ready, 1)

                if back is not None:
                    act.wait_ge(y_affine_ready, u)
                    for t in range(T):
                        nc.scalar.activation(kt_or_y[:, t, :], kt_or_y[:, t, :], ACT.Identity, bias=y_add[:, t:t + 1],
                                             scale=y_rstd[:, t:t + 1]).then_inc(yh_ready, 1)
                if prep:
                    split_high(1, K_ if prep == 1 else Q_)
                if front is not None:
                    act.wait_ge(k_shift_ready, u + 1)
                    for i in range(C):
                        nc.scalar.activation(k_or_qt[:, i, :], k_or_qt[:, i, :], ACT.Exp, bias=k_shift[:, i:i + 1],
                                             accum_out=k_sum[:, i:i + 1]).then_inc(k_exp, 1)

                def high_k():
                    if not isinstance(u, int) or u:
                        act.wait_ge(qt_hi_ready, 16 * u)
                    for i in range(C):
                        act.wait_ge(k_normed, 4 * u + i + 1)
                        nc.scalar.copy(kq_hi[:, i * S:i * S + S], k_or_qt[:, i, :]).then_inc(k_hi_ready, 1)

                if back is None:
                    high_k()
                if back is not None:
                    act.wait_ge(film_now_ready, u)
                    act.wait_ge(qt_lo_ready, 16 * u)
                    for c in range(C):
                        if c == 2 and front is not None:
                            high_k()
                        act.wait_ge(done["YT"], 4 * (u - 1) + c + 1)
                        if c >= 2:
                            act.wait_ge(h_ready, 4 * (u - 1) + c - 1)
                        turned = nc.scalar.activation(tanh[:, c % 2, :], bank("YT", c), ACT.Tanh, bias=film_now[:, 1, c:c + 1],
                                                      scale=film_now[:, 0, c:c + 1])
                        if front is None:
                            turned.then_inc(film_read, 1)
                            if c:
                                high(c - 1)
                            continue
                        nc.scalar.activation(xh_or_h[:, c, :], bank("YT", c), ACT.Identity, bias=film_now[:, 3, c:c + 1],
                                             scale=film_now[:, 2, c:c + 1]).then_inc(film_read, 1)
                    for c in range(C) if front is not None else (C - 1,):
                        high(c)
                if front is not None:
                    for t in range(T):
                        act.wait_ge(v_biased, 4 * u + t + 1)
                        nc.scalar.copy(v_hi[:, t, :], v[:, t, :]).then_inc(v_hi_ready, 1)
                if following is not None:
                    normalise_x(u + 1, following, u if back is not None else None)
                if front is not None:
                    for t in range(T):
                        act.wait_ge(q_centred, 4 * u + t + 1)
                        nc.scalar.activation(q[:, t, :], q[:, t, :], ACT.Exp).then_inc(q_exp, 1)
                        if t == 0:
                            act.wait_ge(kt_hi_ready, 16 * (u + 1))
                        act.wait_ge(q_exp, 4 * u + t + 1)
                        nc.scalar.activation(kq_hi[:, t * D:t * D + D], q[:, t, :], ACT.Copy, scale=ONE).then_inc(q_hi_ready, 1)
                    act.wait_ge(att_ready, u + 1)
                    nc.scalar.copy(att_hi[:], att[:]).then_inc(att_hi_ready, 1)
                if following is not None:
                    turned_x(u + 1, following)
                if isinstance(u, int) and u == 0:
                    split_high(0, O_)
                if prep:
                    split_high(1, V_ if prep == 1 else O_)

            act.wait_ge(consts_ready, 1)
            nc.scalar.activation(warm[:], minus_half[:, 0:1], ACT.Tanh)
            act.wait_ge(emb_loaded, 16)
            nc.scalar.activation(emb_tanh[:], emb[:], ACT.Tanh, scale=0.5).then_inc(emb_tanh_ready, 1)
            normalise_x(0, 0, None)
            split_high(0, K_)
            act.wait_ge(ln_ready, 2)
            turned_x(0, 0)
            split_high(0, V_)
            split_high(0, Q_)
            step(0, 0, None, 0)
            with act.Fori(1, B - 1) as u:
                step(u, 0, 0, 0)
            act.wait_ge(ln_ready, 4)
            step(B - 1, 0, 0, 1, prep=1)
            step(B, 1, 0, 1, prep=2)
            with act.Fori(B + 1, UNITS - 1) as u:
                step(u, 1, 1, 1)
            step(UNITS - 1, 1, 1, None)
            step(UNITS, None, 1, None)

        @block.gpsimd
        def _(pool):
            def x_power(unit):
                pool.wait_ge(x_var_ready, unit + 1)
                nc.gpsimd.tensor_tensor(x_rstd[:], x_var[:], minus_half[:], ALU.pow).then_inc(x_rstd_ready, 1)

            def y_power(u):
                pool.wait_ge(y_var_ready, u + 1)
                nc.gpsimd.tensor_tensor(y_rstd[:], y_var[:], minus_half[:], ALU.pow).then_inc(y_rstd_ready, 1)

            def x_low_part(unit):
                for c in range(C):
                    pool.wait_ge(xt_hi_ready, 4 * unit + c + 1)
                    nc.gpsimd.tensor_tensor(xt_lo[:, c, :], xh_or_h[:, c, :], xt_hi[:, c, :], ALU.subtract).then_inc(xt_lo_ready, 1)

            def v_low_part(u):
                for t in range(T):
                    pool.wait_ge(v_hi_ready, 4 * u + t + 1)
                    nc.gpsimd.tensor_tensor(v_lo[:, t, :], v[:, t, :], v_hi[:, t, :], ALU.subtract).then_inc(v_lo_ready, 1)

            def att_low_part(u):
                pool.wait_ge(att_hi_ready, u + 1)
                nc.gpsimd.tensor_tensor(att_lo[:], att[:], att_hi[:], ALU.subtract).then_inc(att_lo_ready, 1)

            def add_bias(unit, layer):
                b = batch(unit, layer)
                pool.wait_ge(xh_ready, 4 * (unit + 1))
                nc.gpsimd.tensor_tensor(xu(b), xu(b), bias_o[:].unsqueeze(1).broadcast_to([P, T, D]), ALU.add
                                        ).then_inc(x_biased, 1)

            def prepare_w(layer, m):
                pool.wait_ge(w_peak, 4 * layer + m + 1)
                nc.gpsimd.partition_all_reduce(peak_all[:, layer, m:m + 1], peak[:, layer, m:m + 1], P, RMAX).then_inc(w_peak_all, 1)

            def split_low(m):
                for c in range(C):
                    pool.wait_ge(w_hi_ready, 4 * (4 + m) + c + 1)
                    last = nc.gpsimd.tensor_tensor(w_lo[HELD[1][m]][:, c, :], stages[1][m][:, c, :], w_hi[HELD[1][m]][:, c, :],
                                                   ALU.subtract)
                last.then_inc(w_ready[1], 1)

            def prepare_ln(layer):
                pool.wait_ge(ln_peak, layer + 1)
                nc.gpsimd.partition_all_reduce(peak_all[:, layer, LN:LN + 1], peak[:, layer, LN:LN + 1], P, RMAX).then_inc(ln_peak_all, 1)

            def prepare_film(layer):
                pool.wait_ge(film_peak, layer + 1)
                nc.gpsimd.partition_all_reduce(peak_all[:, layer, 6:7], peak[:, layer, 6:7], P, RMAX).then_inc(film_peak_all, 1)

            def step(u, front, back, following, prep=None):
                if prep:
                    prepare_w(1, K_ if prep == 1 else Q_)
                if prep:
                    split_low(K_ if prep == 1 else Q_)
                if following is not None:
                    x_power(u + 1)
                if back is not None:
                    hi, lo = (ht_hi, ht_lo) if front is not None else (last_ht_hi, last_ht_lo)
                    for c in range(C):
                        pool.wait_ge(ht_hi_ready, 4 * (u - 1) + c + 1)
                        nc.gpsimd.tensor_tensor(lo[:, c, :], xh_or_h[:, c, :], hi[:, c, :], ALU.subtract
                                                ).then_inc(ht_lo_ready, 1)
                if front is not None:
                    v_low_part(u)
                if prep == 1:
                    pool.wait_ge(bias_o1_loaded, 16)
                if following is not None:
                    add_bias(u + 1, following)
                if front is not None:
                    att_low_part(u)
                if prep == 1:
                    prepare_w(1, V_)
                if prep == 2:
                    prepare_film(1)
                if following is not None:
                    x_low_part(u + 1)
                if prep == 2:
                    prepare_w(1, O_)
                if front is not None:
                    y_power(u)
                if prep:
                    split_low(V_ if prep == 1 else O_)

            pool.wait_ge(consts_ready, 1)
            x_power(0)
            prepare_ln(0)
            prepare_w(0, K_)
            prepare_w(0, V_)
            prepare_w(0, Q_)
            x_power(1)
            pool.wait_ge(row_bias_loaded[0], 48)
            add_bias(0, 0)
            prepare_ln(1)
            v_low_part(0)
            prepare_w(0, O_)
            add_bias(1, 0)
            att_low_part(0)
            x_low_part(1)
            y_power(0)
            prepare_film(0)
            with pool.Fori(1, B - 1) as u:
                step(u, 0, 0, 0)
            step(B - 1, 0, 0, 1, prep=1)
            step(B, 1, 0, 1, prep=2)
            with pool.Fori(B + 1, UNITS - 1) as u:
                step(u, 1, 1, 1)
            step(UNITS - 1, 1, 1, None)
            step(UNITS, None, 1, None)


_W = (("L0_cond_Wk", "L0_cond_Wv", "L0_cond_Wq", "L0_cond_W_out"),
      ("L1_cond_Wk", "L1_cond_Wv", "L1_cond_Wq", "L1_cond_film_out_W"))
_ROWS = (("L0_cond_bv", "L0_cond_bq", "L0_cond_b_out"),
         ("L1_cond_bv", "L1_cond_bq", "L1_cond_film_out_b"))
_WEMB = ("L0_cond_W_emb", "L1_cond_film_emb_W")
_COLS = (("L0_cond_ln_w", "L0_cond_ln_b", "L0_cond_bk", "L0_cond_ln2_w", "L0_cond_ln2_b", "L0_cond_b_emb"),
         ("L1_cond_norm_scale", "L1_cond_norm_bias", "L1_cond_bk", "L1_cond_film_norm_scale",
          "L1_cond_film_norm_bias", "L1_cond_film_emb_b"))


def kernel(**inputs):
    import numpy as np
    import concourse.bacc as bacc
    from concourse.bass_utils import run_bass_kernel_spmd

    a = {k: np.ascontiguousarray(v) for k, v in inputs.items()}

    def by_partition(rows, n):
        rows = rows.reshape(*rows.shape[:-1], n, P)
        return np.ascontiguousarray(np.moveaxis(rows, -1, 0))

    mask0 = a["mask_BxSx1_fk1"].reshape(B, S)
    mask1 = a["mask_BxS_ik0"].reshape(B, S)
    arrays = {
        "x": a["x"], "mask0": mask0, "mask1": mask1,
        "emb": np.ascontiguousarray(by_partition(a["cond_2048"], KE).transpose(0, 2, 1)),
        "cols": np.stack([np.concatenate([by_partition(a[n], a[n].size // P) for n in names], 1) for names in _COLS], 1),
        "ident": np.eye(P, dtype=np.float32),
        "blocks": 1 / ONE * np.stack([np.kron(np.eye(P * h // D), np.ones((D // h, D // h))) for h in HEADS], 1).astype(np.float32),
    }
    for names in (*_W, *_ROWS, _WEMB):
        for n in names:
            arrays[n] = a[n]
    nc = bacc.Bacc("TRN2", target_bir_lowering=False, num_devices=1)
    arrays = {f"in_{k}": np.ascontiguousarray(v) for k, v in arrays.items()}
    ap = {k[3:]: nc.dram_tensor(k, v.shape, mybir.dt.from_np(v.dtype), kind="ExternalInput").ap() for k, v in arrays.items()}
    out = nc.dram_tensor("out_0", (B, S, D), F32, kind="ExternalOutput").ap()
    build(nc, ap["x"], ap["emb"], ap["mask0"], ap["mask1"],
          [[ap[n] for n in names] for names in _W], [[ap[n] for n in names] for names in _ROWS],
          [ap[n] for n in _WEMB], ap["cols"], ap["ident"], ap["blocks"], out)
    r = run_bass_kernel_spmd(nc, [arrays], core_ids=[0])
    return r.results[0]["out_0"]
```
